# Optimizing a Trainium2 kernel written in Bass

```python
import numpy as np
import jax
import jax.numpy as jnp

def _softmax(x, axis=-1):
    return jax.nn.softmax(x, axis=axis)

def _gelu(x):
    return jax.nn.gelu(x, approximate=True)

def _silu(x):
    return jax.nn.silu(x)

def _sigmoid(x):
    return jax.nn.sigmoid(x)

def _layernorm(x, axis=-1, eps=1e-05):
    m = jnp.mean(x, axis=axis, keepdims=True)
    v = jnp.var(x, axis=axis, keepdims=True)
    return (x - m) / jnp.sqrt(v + eps)

def _scatter_add(tgt, idx, src, axis=0):
    return tgt.at[idx].add(src)

def _segment_sum(src, seg, n):
    return jax.ops.segment_sum(src, seg, n)
kernel_name = 'mk_conv_preact_d1_conv_nchw128_r2_c775bd'

def setup_inputs(seed: int=0):
    np.random.seed(seed)
    _w = jnp.asarray

    def _rec_inputs():
        import jax
        import jax.numpy as jnp
        _gk = jax.random.key(seed)
        x = -0.0002091 + 1 * jax.random.normal(jax.random.fold_in(_gk, 1), (32, 64, 56, 56), jnp.float32)
        return x
    x = _rec_inputs()

    def _L0_conv_setup():
        import jax, jax.numpy as jnp
        import numpy as np
        from jax import lax
        BN_EPS = 1e-05
        W_BITS = 8

        def quantize_weight(w, bits):
            qmax = 2.0 ** (bits - 1) - 1.0
            scale = jnp.max(jnp.abs(w)) / qmax
            wq = jnp.round(w / scale) * scale
            return w + lax.stop_gradient(wq - w)

        def conv3x3(x, w, b):
            y = lax.conv_general_dilated(x, w, window_strides=(1, 1), padding=((1, 1), (1, 1)), dimension_numbers=('NCHW', 'OIHW', 'NCHW'))
            return y + b[None, :, None, None]

        def batchnorm(x, gamma, beta):
            mu = jnp.mean(x, axis=(0, 2, 3), keepdims=True)
            var = jnp.var(x, axis=(0, 2, 3), keepdims=True)
            xhat = (x - mu) * lax.rsqrt(var + BN_EPS)
            return gamma[None, :, None, None] * xhat + beta[None, :, None, None]
        key = jax.random.key(seed)
        ks = jax.random.split(key, 5)
        N, C, H, W = (32, 64, 56, 56)
        x = jax.random.normal(ks[0], (N, C, H, W), dtype=jnp.float32)
        w1 = jax.random.normal(ks[1], (C, C, 3, 3), dtype=jnp.float32) * 0.05
        b1 = jax.random.normal(ks[2], (C,), dtype=jnp.float32) * 0.01
        w2 = jax.random.normal(ks[3], (C, C, 3, 3), dtype=jnp.float32) * 0.05
        b2 = jax.random.normal(ks[4], (C,), dtype=jnp.float32) * 0.01
        return {'x': x, 'w1': w1, 'b1': b1, 'gamma1': jnp.ones((C,), jnp.float32), 'beta1': jnp.zeros((C,), jnp.float32), 'w2': w2, 'b2': b2, 'gamma2': jnp.ones((C,), jnp.float32), 'beta2': jnp.zeros((C,), jnp.float32)}
    _L0_conv_all = _L0_conv_setup()
    _L0_conv_in = {k: v for k, v in _L0_conv_all.items() if k in ('w1', 'b1', 'gamma1', 'beta1', 'w2', 'b2', 'gamma2', 'beta2')}
    del _L0_conv_all
    return {'x': x, 'L0_conv_w1': _L0_conv_in['w1'], 'L0_conv_b1': _L0_conv_in['b1'], 'L0_conv_gamma1': _L0_conv_in['gamma1'], 'L0_conv_beta1': _L0_conv_in['beta1'], 'L0_conv_w2': _L0_conv_in['w2'], 'L0_conv_b2': _L0_conv_in['b2'], 'L0_conv_gamma2': _L0_conv_in['gamma2'], 'L0_conv_beta2': _L0_conv_in['beta2']}

def reference(x, L0_conv_w1, L0_conv_b1, L0_conv_gamma1, L0_conv_beta1, L0_conv_w2, L0_conv_b2, L0_conv_gamma2, L0_conv_beta2):
    import jax
    import jax.numpy as jnp

    def _L0_conv_ref(x, w1, b1, gamma1, beta1, w2, b2, gamma2, beta2):
        import jax, jax.numpy as jnp
        import numpy as np
        from jax import lax
        BN_EPS = 1e-05
        W_BITS = 8

        def quantize_weight(w, bits):
            qmax = 2.0 ** (bits - 1) - 1.0
            scale = jnp.max(jnp.abs(w)) / qmax
            wq = jnp.round(w / scale) * scale
            return w + lax.stop_gradient(wq - w)

        def conv3x3(x, w, b):
            y = lax.conv_general_dilated(x, w, window_strides=(1, 1), padding=((1, 1), (1, 1)), dimension_numbers=('NCHW', 'OIHW', 'NCHW'))
            return y + b[None, :, None, None]

        def batchnorm(x, gamma, beta):
            mu = jnp.mean(x, axis=(0, 2, 3), keepdims=True)
            var = jnp.var(x, axis=(0, 2, 3), keepdims=True)
            xhat = (x - mu) * lax.rsqrt(var + BN_EPS)
            return gamma[None, :, None, None] * xhat + beta[None, :, None, None]
        identity = x
        out = conv3x3(x, quantize_weight(w1, W_BITS), b1)
        out = jax.nn.relu(batchnorm(out, gamma1, beta1))
        out = conv3x3(out, quantize_weight(w2, W_BITS), b2)
        out = batchnorm(out, gamma2, beta2)
        out = jax.nn.relu(out + identity)
        return out

    def _gn(v, G=32, eps=1e-05):
        B_, C_, H_, W_ = v.shape
        g = v.reshape(B_, G, C_ // G, H_, W_)
        m = jnp.mean(g, axis=(2, 3, 4), keepdims=True)
        s = jnp.var(g, axis=(2, 3, 4), keepdims=True)
        return ((g - m) / jnp.sqrt(s + eps)).reshape(v.shape)

    def _ln_c(v, eps=1e-06):
        m = jnp.mean(v, axis=1, keepdims=True)
        s = jnp.var(v, axis=1, keepdims=True)
        return (v - m) / jnp.sqrt(s + eps)

    def _ln_t(v, eps=1e-05):
        m = jnp.mean(v, axis=-1, keepdims=True)
        s = jnp.var(v, axis=-1, keepdims=True)
        return (v - m) / jnp.sqrt(s + eps)

    def _to_tokens(v):
        B_, C_, H_, W_ = v.shape
        return v.reshape(B_, C_, H_ * W_).transpose(0, 2, 1)

    def _from_tokens(t, like):
        B_, C_, H_, W_ = like.shape
        return t.transpose(0, 2, 1).reshape(B_, C_, H_, W_)
    x = x + _L0_conv_ref(_gn(x), L0_conv_w1, L0_conv_b1, L0_conv_gamma1, L0_conv_beta1, L0_conv_w2, L0_conv_b2, L0_conv_gamma2, L0_conv_beta2)
    return x

_drawn_inputs = setup_inputs


def setup_inputs(seed=0):
    import zlib

    import numpy as np

    out = dict(_drawn_inputs(seed))
    spreads = {'L0_conv_gamma1': (1.0, 0.2),
     'L0_conv_beta1': (0.0, 0.1),
     'L0_conv_gamma2': (1.0, 0.2),
     'L0_conv_beta2': (0.0, 0.1)}
    factors = {}
    for name, (base, spread) in spreads.items():
        noise = np.random.default_rng([zlib.crc32(name.encode()), seed]).standard_normal(out[name].shape)
        drawn = base * np.exp(spread * noise) if base else spread * noise
        out[name] = jnp.asarray(drawn.astype(out[name].dtype))
    for name, factor in factors.items():
        out[name] = (out[name] * factor).astype(out[name].dtype)
    return out
```

```python
from contextlib import ExitStack

import concourse.bass as bass
from concourse import mybir

F32 = mybir.dt.float32
F16 = mybir.dt.float16
BF16 = mybir.dt.bfloat16
U32 = mybir.dt.uint32
ALU = mybir.AluOpType
ACT = mybir.ActivationFunctionType
AX = mybir.AxisListType

P = 128
BODY = 4
GN_EPS = 1e-5
BN_EPS = 1e-5
QMAX = 127.0
ROUND = 12582912.0
GN_SCALE = 512.0
BN_SCALE = 64.0


def conv_block_kernel(nc, x, w1, b1, g1, be1, w2, b2, g2, be2, out):
    NIMG, C, H, W = x.shape
    assert C == 64 and H % 2 == 0
    J = H // 2
    KB = J + 1
    WP = W + 2
    PIX = J * W
    ROWS_PER_BANK = 7
    NCH = J // ROWS_PER_BANK
    CH = ROWS_PER_BANK * W
    NPAIR = NCH // 2
    HALF = 2 * ROWS_PER_BANK + 1
    DIRECT = (3, 1)
    assert NPAIR == 2 and J % (2 * ROWS_PER_BANK) == 0 and NIMG % BODY == 0 and CH <= 512
    RES = 20
    SPILL = NIMG - RES
    assert RES % BODY == 0 and SPILL % BODY == 0 and SPILL <= RES - 2 * BODY + BODY
    GRP = 2

    with ExitStack() as ctx:
        def sb(name, shape, dt):
            return ctx.enter_context(nc.sbuf_tensor(name, shape, dt))

        def psum(name, shape, dt):
            return ctx.enter_context(nc.psum_tensor(name, shape, dt))

        def sem(name):
            return ctx.enter_context(nc.semaphore(name))

        y1_spill = nc.dram_tensor("y1_spill", [SPILL, P, PIX], F32, kind="Internal").ap()
        y2_spill = nc.dram_tensor("y2_spill", [SPILL, C, H, W], F32, kind="Internal").ap()

        slots_sb = sb("slots_sb", [P, RES * KB, W], F32)
        xin = sb("xin", [P, 4, KB, W], F32)
        act = sb("act", [P, 2, KB, W], F32)
        hi = sb("hi", [P, 2, KB, WP], F16)
        lo = sb("lo", [P, 2, KB, WP], F16)
        stage = sb("stage", [P, 2, J, W], F32)
        wmat = [sb(f"wmat{n}", [P, 3, 2, P], BF16) for n in (1, 2)]
        wraw = [sb(f"wraw{n}", [P, C * 9], F32) for n in (1, 2)]
        wpad = [sb(f"wpad{n}", [C, 3, 5, C], BF16) for n in (1, 2)]
        ident = sb("ident", [C, C], BF16)
        same_channel = sb("same_channel", [P, P], F32)
        gn_avg = sb("gn_avg", [P, P], F32)
        bn_avg = sb("bn_avg", [P, P], F32)
        par = sb("par", [P, 6], F32)
        wstat = sb("wstat", [P, 8], F32)
        qscale = sb("qscale", [P, 2], F32)
        evac_scale = sb("evac_scale", [P, 2], F32)
        pow2 = sb("pow2", [P, 2], F32)
        pabs = sb("pabs", [P, 2], F32)
        warm = sb("warm", [C, 1], F32)
        gn_tup = sb("gn_tup", [P, 2, 4, 6], F32)
        gn_mv = sb("gn_mv", [P, 2, 2], F32)
        gn_sq = sb("gn_sq", [P, 2], F32)
        gn_g = sb("gn_g", [P, 2, 2], F32)
        gn_var = sb("gn_var", [P, 2], F32)
        gn_sd = sb("gn_sd", [P, 2], F32)
        gn_tmp = sb("gn_tmp", [P, 4, 2], F32)
        gn_s = sb("gn_s", [P, 2], F32)
        gn_b = sb("gn_b", [P, 2], F32)
        gn_s_all = sb("gn_s_all", [P, NIMG], F32)
        gn_b_all = sb("gn_b_all", [P, NIMG], F32)
        skip_s = sb("skip_s", [P, NIMG], F32)
        skip_b = sb("skip_b", [P, NIMG], F32)
        bn_tup = sb("bn_tup", [P, BODY * NCH, 6], F32)
        bn_mv = sb("bn_mv", [P, 2], F32)
        bn_sq = sb("bn_sq", [P, 1], F32)
        bn_acc = [sb(f"bn_acc{n}", [P, 2], F32) for n in (1, 2)]
        bn_w = sb("bn_w", [P, 2, 10], F32)
        bn_affine = sb("bn_affine", [P, 2, 2], F32)
        bn_sd = sb("bn_sd", [P, 2], F32)

        conv_ps = psum("conv_ps", [P, 4, 512], F32)
        stat_ps = psum("stat_ps", [P, 512], F32)
        wt_ps = [psum(f"wt_ps{n}", [P, 3, 2, P], BF16) for n in (1, 2)]

        params_loaded = sem("params_loaded")
        weights_loaded = [sem(f"weights_loaded{n}") for n in (1, 2)]
        masks_zeroed = sem("masks_zeroed")
        masks_made = sem("masks_made")
        pads_zeroed = sem("pads_zeroed")
        wprep = sem("wprep")
        absmax_ready = sem("absmax_ready")
        absmax_all = sem("absmax_all")
        quantised = sem("quantised")
        transposed = sem("transposed")
        wmat_ready = sem("wmat_ready")
        evac_scale_ready = sem("evac_scale_ready")
        averages_made = sem("averages_made")
        x0_first_rows = sem("x0_first_rows")
        x_loaded = [sem(f"x_loaded{b}") for b in range(4)]
        gn_tuples = sem("gn_tuples")
        gn_step_a = sem("gn_step_a")
        gn_moments = sem("gn_moments")
        gn_combined = sem("gn_combined")
        gn_step_b = sem("gn_step_b")
        gn_copied = sem("gn_copied")
        gn_var_ready = sem("gn_var_ready")
        gn_sd_ready = sem("gn_sd_ready")
        gn_coef_ready = sem("gn_coef_ready")
        half_act = [sem(f"half_act{n}") for n in (1, 2)]
        half_hi = [sem(f"half_hi{n}") for n in (1, 2)]
        half_lo = [sem(f"half_lo{n}") for n in (1, 2)]
        act_ready = [sem(f"act_ready{n}") for n in (1, 2)]
        hi_ready = [sem(f"hi_ready{n}") for n in (1, 2)]
        lo_ready = [sem(f"lo_ready{n}") for n in (1, 2)]
        pair_done = [[sem(f"pair_done{n}_{p}") for p in range(2)] for n in (1, 2)]
        pair_evac = [[sem(f"pair_evac{n}_{p}") for p in range(2)] for n in (1, 2)]
        stage_read = [sem(f"stage_read{n}") for n in (1, 2)]
        stage_stored = [[sem(f"stage_stored{n}_{b}") for b in range(2)] for n in (1, 2)]
        bn_tuples = [sem(f"bn_tuples{n}") for n in (1, 2)]
        bn_step = [sem(f"bn_step{n}") for n in (1, 2)]
        bn_sums = [sem(f"bn_sums{n}") for n in (1, 2)]
        bn_combined = [sem(f"bn_combined{n}") for n in (1, 2)]
        bn_chain = [sem(f"bn_chain{n}") for n in (1, 2)]
        bn_var_ready = [sem(f"bn_var_ready{n}") for n in (1, 2)]
        bn_sd_ready = [sem(f"bn_sd_ready{n}") for n in (1, 2)]
        bn_coef_ready = [sem(f"bn_coef_ready{n}") for n in (1, 2)]
        y1_loaded = [sem(f"y1_loaded{b}") for b in range(4)]
        skip_coef = sem("skip_coef")
        x3_loaded = [sem(f"x3_loaded{b}") for b in range(4)]
        y2_loaded = [sem(f"y2_loaded{b}") for b in range(4)]
        u_ready = sem("u_ready")
        sum_ready = sem("sum_ready")
        out_ready = sem("out_ready")
        out_stored = [sem(f"out_stored{b}") for b in range(4)]

        A1, B1, A2, B2 = (bn_w[:, n, c:c + 1] for n in (0, 1) for c in (8, 9))

        def odd_even(ap):
            return ap.rearrange("c (j h) w -> h c j w", h=2)

        def run_slots(eng, start, stop, body):
            n = (stop - start) // BODY
            if n >= 2 and (stop - start) % BODY == 0:
                with eng.Fori(0, n) as it:
                    for k in range(BODY):
                        body(it * BODY + (start + k), start + k)
            else:
                for i in range(start, stop):
                    body(i, i)

        def image_of(q, r):
            return q if r < SPILL else q + SPILL if r < RES else q - RES + SPILL

        third = (J - 1) // 3
        cut = 1 + 2 * third

        ubuf = [act[:, 0, 0:J, :], act[:, 1, 0:J, :], stage[:, 0], stage[:, 1]]

        PADS_W0, PADS_0, PADS_1, PADS = 1, 6, 11, 12
        MASKS = 4

        block = ctx.enter_context(nc.Block())

        @block.sync
        def _(sp):
            def load_x(j, r):
                b = r % 4
                if r >= 4:
                    sp.wait_ge(act_ready[0], j - 3)
                    if r - 4 < DIRECT[0]:
                        sp.wait_ge(half_lo[0], j - 3)
                src = odd_even(x[j])
                if r == 0:
                    sp.dma_start(xin[0:C, b, 1:cut, :], src[1][:, 0:cut - 1, :]).then_inc(x0_first_rows, 16)
                    sp.dma_start(xin[C:P, b, 0:cut, :], src[0][:, 0:cut, :]).then_inc(x0_first_rows, 16)
                    sp.dma_start(xin[0:C, b, cut:KB, :], src[1][:, cut - 1:J, :]).then_inc(x_loaded[b], 16)
                    sp.dma_start(xin[C:P, b, cut:J, :], src[0][:, cut:J, :]).then_inc(x_loaded[b], 16)
                    return
                sp.dma_start(xin[0:C, b, 1:KB, :], src[1]).then_inc(x_loaded[b], 16)
                sp.dma_start(xin[C:P, b, 0:J, :], src[0]).then_inc(x_loaded[b], 16)

            for h in range(2):
                sp.dma_start(wraw[0][C * h:C * h + C, :], w1.rearrange("o i a b -> o (i a b)")).then_inc(weights_loaded[0], 16)
            for j in range(3):
                load_x(j, j)
            for col, v in enumerate((b1, g1, be1, b2, g2, be2)):
                for h in range(2):
                    sp.dma_start(par[C * h:C * h + C, col:col + 1], v.rearrange("(c a) -> c a", a=1)).then_inc(params_loaded, 16)
            for j in range(3, 6):
                load_x(j, j)
            for h in range(2):
                sp.dma_start(wraw[1][C * h:C * h + C, :], w2.rearrange("o i a b -> o (i a b)")).then_inc(weights_loaded[1], 16)

            def pass1(i, r):
                if r + 6 < NIMG:
                    load_x(i + 6, r + 6)
                b = r % 2
                sp.wait_ge(pair_evac[0][1], i + 1)
                done = stage_stored[0][b]
                if r < SPILL:
                    for h in range(2):
                        sp.dma_start(y1_spill[i, C * h:C * h + C, :],
                                     stage[C * h:C * h + C, b].rearrange("p j w -> p (j w)")).then_inc(done, 16)
                else:
                    base = (i - SPILL) * KB
                    sp.dma_start(slots_sb[0:C, bass.ds(base + 1, J), :], stage[C:P, b]).then_inc(done, 16)
                    sp.dma_start(slots_sb[C:P, bass.ds(base, J), :], stage[0:C, b]).then_inc(done, 16)

            run_slots(sp, 0, BODY, pass1)
            run_slots(sp, BODY, SPILL, pass1)
            run_slots(sp, SPILL, NIMG - 2 * BODY, pass1)
            run_slots(sp, NIMG - 2 * BODY, NIMG - BODY, pass1)
            run_slots(sp, NIMG - BODY, NIMG, pass1)
            for b in range(2):
                sp.wait_ge(stage_stored[0][b], 16 * NIMG)

            def load_y1(p, r):
                b = r % 4
                base = (p - RES) * KB
                img = p - RES
                sp.dma_start(slots_sb[0:C, bass.ds(base + 1, J), :],
                             y1_spill[img, C:P, :].rearrange("p (j w) -> p j w", w=W)).then_inc(y1_loaded[b], 16)
                sp.dma_start(slots_sb[C:P, bass.ds(base, J), :],
                             y1_spill[img, 0:C, :].rearrange("p (j w) -> p j w", w=W)).then_inc(y1_loaded[b], 16)

            def load_x3(q, r, img):
                b = r % 4
                if r >= 4:
                    sp.wait_ge(out_ready, q - 3)
                src = x[img].rearrange("c (h r) w -> h c r w", h=2)
                for h in range(2):
                    sp.dma_start(xin[C * h:C * h + C, b, 0:J, :], src[h]).then_inc(x3_loaded[b], 16)

            def pass2(i, r):
                if RES <= r + 4 < NIMG:
                    sp.wait_ge(act_ready[1], i + 1)
                    load_y1(i + 4, r + 4)
                b = r % 2
                sp.wait_ge(pair_evac[1][1], i + 1)
                done = stage_stored[1][b]
                if r < SPILL:
                    dst = odd_even(y2_spill[i])
                    for h in range(2):
                        for part in range(2):
                            sp.dma_start(dst[h][:, part * J // 2:(part + 1) * J // 2, :],
                                         stage[C * h:C * h + C, b, part * J // 2:(part + 1) * J // 2]).then_inc(done, 16)
                else:
                    base = (i if r < RES else i - RES) * KB
                    for h in range(2):
                        for part in range(2):
                            sp.dma_start(
                                slots_sb[C * part:C * part + C, bass.ds(base + h, J // 2, 2), :],
                                stage[C * h:C * h + C, b, part * J // 2:(part + 1) * J // 2]).then_inc(done, 16)

            run_slots(sp, 0, SPILL, pass2)
            run_slots(sp, SPILL, RES - BODY, pass2)
            run_slots(sp, RES - BODY, RES, pass2)
            sp.wait_ge(act_ready[0], NIMG)
            for q in range(4):
                load_x3(q, q, q)
            run_slots(sp, RES, NIMG - BODY, pass2)
            run_slots(sp, NIMG - BODY, NIMG, pass2)
            for b in range(2):
                sp.wait_ge(stage_stored[1][b], 32 * NIMG)

            def store_out(q, r):
                sp.wait_ge(out_ready, q + 1)
                dst = out[image_of(q, r)].rearrange("c (h r) w -> h c r w", h=2)
                for h in range(2):
                    sp.dma_start(dst[h], ubuf[r % 4][C * h:C * h + C]).then_inc(out_stored[r % 4], 16)

            def pass3(q, r):
                n, m = q + 4, r + 4
                load_x3(n, m, image_of(n, m))
                if m >= RES:
                    for h in range(2):
                        sp.dma_start(slots_sb[C * h:C * h + C, bass.ds((n - RES) * KB, J), :],
                                     y2_spill[n - RES].rearrange("c (h r) w -> h c r w", h=2)[h]).then_inc(y2_loaded[m % 4], 16)
                store_out(q, r)

            for start, stop in ((0, SPILL - 4), (SPILL - 4, SPILL), (SPILL, RES - 4), (RES - 4, RES), (RES, NIMG - 4)):
                run_slots(sp, start, stop, pass3)
            for q in range(NIMG - 4, NIMG):
                store_out(q, q)
            for b in range(4):
                sp.wait_ge(out_stored[b], 8 * NIMG)

        @block.gpsimd
        def _(pool):
            nc.gpsimd.memset(ident[:, :], 0.0).then_inc(masks_zeroed, 1)
            nc.gpsimd.memset(same_channel[:, :], 0.0).then_inc(masks_zeroed, 1)
            made = zeroed = reduced = 0

            def cores_together():
                for semaphore, count in ((pads_zeroed, zeroed), (masks_made, made), (absmax_all, reduced)):
                    if count:
                        pool.wait_ge(semaphore, count)

            def zero(*paddings):
                nonlocal zeroed
                for padding in paddings:
                    cores_together()
                    nc.gpsimd.memset(padding, 0.0).then_inc(pads_zeroed, 1)
                    zeroed += 1

            def diagonal(m, pattern, base, fill):
                nonlocal made
                cores_together()
                nc.gpsimd.affine_select(out=m, in_=m, compare_op=ALU.not_equal, fill=fill, base=base,
                                        pattern=pattern, channel_multiplier=1).then_inc(masks_made, 1)
                made += 1

            def largest(n):
                nonlocal reduced
                cores_together()
                pool.wait_ge(absmax_ready, n + 1)
                nc.gpsimd.partition_all_reduce(wstat[:, n + 2:n + 3], wstat[:, n:n + 1], P,
                                               bass.bass_isa.ReduceOp.max).then_inc(absmax_all, 1)
                reduced += 1

            zero(wpad[0][:, :, 0:5:4, :])
            pool.wait_ge(masks_zeroed, 2)
            diagonal(ident[:, :], [[-1, C]], 0, 1.0)
            for other_half in (0, C, -C):
                diagonal(same_channel[:, :], [[-1, P]], other_half, 0.5 / GRP)
            assert made == MASKS
            largest(0)
            for n in range(2):
                zero(hi[:, n, :, 0:WP:WP - 1], lo[:, n, :, 0:WP:WP - 1], act[0:C, n, 0, :], act[C:P, n, KB - 1, :],
                     hi[0:C, n, 0, :])
                assert zeroed == (PADS_0, PADS_1)[n]
            zero(wpad[1][:, :, 0:5:4, :])
            assert zeroed == PADS
            largest(1)

        @block.scalar
        def _(sc):
            def split_hi(ph, i, r):
                k = r % 2
                sc.wait_ge(act_ready[ph], i + 1)
                if r >= 2:
                    sc.wait_ge(pair_done[ph][1], i - 1)
                nc.scalar.copy(hi[:, k, :, 1:1 + W], act[:, k]).then_inc(hi_ready[ph], 1)

            def normalise(ph, i, r, rows, func, scale, bias):
                k = r % 2
                if r >= 2:
                    sc.wait_ge(lo_ready[ph], i - 1)
                nc.scalar.activation(act[:, k, 1:J, :], rows(0, P, 1, J), func, bias=bias(0, P), scale=scale(0, P))
                nc.scalar.activation(act[C:P, k, 0, :], rows(C, P, 0, 1), func, bias=bias(C, P), scale=scale(C, P))
                nc.scalar.activation(act[0:C, k, J, :], rows(0, C, J, KB), func, bias=bias(0, C),
                                     scale=scale(0, C)).then_inc(act_ready[ph], 1)

            def halves(ph, i, func, rows, scale, bias):
                k = i % 2
                if i >= 2:
                    sc.wait_ge(pair_done[ph][1], i - 1)
                nc.scalar.activation(hi[C:P, k, 0, 1:1 + W], rows(C, P, 0, 1), func, bias=bias(C, P), scale=scale(C, P))
                nc.scalar.activation(hi[:, k, 1:HALF, 1:1 + W], rows(0, P, 1, HALF), func, bias=bias(0, P),
                                     scale=scale(0, P)).then_inc(half_hi[ph], 1)
                if i >= 2:
                    sc.wait_ge(lo_ready[ph], i - 1)
                nc.scalar.activation(act[:, k, HALF:J, :], rows(0, P, HALF, J), func, bias=bias(0, P), scale=scale(0, P))
                nc.scalar.activation(act[0:C, k, J, :], rows(0, C, J, KB), func, bias=bias(0, C),
                                     scale=scale(0, C)).then_inc(act_ready[ph], 1)
                sc.wait_ge(act_ready[ph], i + 1)
                nc.scalar.copy(hi[:, k, HALF:KB, 1:1 + W], act[:, k, HALF:KB]).then_inc(hi_ready[ph], 1)

            def x_args(r):
                m = r % 2

                def rows(a, b, k0, k1):
                    ap = xin[a:b, r % 4, k0:k1, :]
                    return ap.rearrange("p k w -> p (k w)") if k1 - k0 == 1 else ap
                return rows, lambda a, b: gn_s[a:b, m:m + 1], lambda a, b: gn_b[a:b, m:m + 1]

            def halves_x(i):
                sc.wait_ge(gn_coef_ready, i + 1 if i < 2 else i + 2)
                rows, scale, bias = x_args(i)
                halves(0, i, ACT.Identity, rows, scale, bias)

            def normalise_x(i, r):
                m = r % 2
                sc.wait_ge(gn_coef_ready, i + 2 - m)
                rows, scale, bias = x_args(r)
                normalise(0, i, r, rows, ACT.Identity, scale, bias)

            def halves_y1():
                sc.wait_ge(stage_stored[0][0], 16 * SPILL + 32)
                halves(1, 0, ACT.Relu, lambda a, b, k0, k1: slots_sb[a:b, k0:k1, :],
                       lambda a, b: A1[a:b, :], lambda a, b: B1[a:b, :])

            def normalise_y1(i, r):
                if r >= RES:
                    sc.wait_ge(y1_loaded[r % 4], i * 8 + (32 - 8 * (r % 4) - 8 * RES))
                else:
                    sc.wait_ge(stage_stored[0][r % 2], (i - r % 2) * 16 + (16 * SPILL + 32))
                base = (i if r < RES else i - RES) * KB
                normalise(1, i, r, lambda a, b, k0, k1: slots_sb[a:b, bass.ds(base + k0, k1 - k0), :],
                          ACT.Relu, lambda a, b: A1[a:b, :], lambda a, b: B1[a:b, :])

            def evacuate(ph, i, r, p):
                b = r % 2
                if p == 0 and r >= 2:
                    sc.wait_ge(stage_stored[ph][b], (i - b) * (16 if ph == 0 else 32))
                    sc.wait_ge(stage_read[ph], i - 1)
                if p == 0 and r < 2 and ph == 1:
                    sc.wait_ge(stage_stored[0][b], 16 * NIMG)
                sc.wait_ge(pair_done[ph][p], i + 1)
                rows = 2 * ROWS_PER_BANK
                nc.scalar.activation(
                    stage[:, b, p * rows:(p + 1) * rows, :].rearrange("q (n j) w -> q n (j w)", n=2),
                    conv_ps[:, 2 * p:2 * p + 2, 0:CH], ACT.Identity, bias=par[:, 3 * ph:3 * ph + 1],
                    scale=evac_scale[:, ph:ph + 1]).then_inc(pair_evac[ph][p], 1)

            def gn_sqrt(i, r):
                sc.wait_ge(gn_var_ready, i + 5)
                nc.scalar.activation(gn_sd[:, :], gn_var[:, :], ACT.Sqrt).then_inc(gn_sd_ready, 2)

            def gn_sqrt_of(m):
                sc.wait_ge(gn_var_ready, m + 1)
                nc.scalar.activation(gn_sd[:, m:m + 1], gn_var[:, m:m + 1], ACT.Sqrt, scale=-1.0).then_inc(gn_sd_ready, 1)

            def pass1(i, r):
                if r + 1 < NIMG:
                    split_hi(0, i + 1, r + 1)
                if r + 2 < NIMG:
                    normalise_x(i + 2, r + 2)
                evacuate(0, i, r, 0)
                if r % 2 == 1 and r + 4 < NIMG:
                    gn_sqrt(i, r)
                evacuate(0, i, r, 1)

            sc.wait_ge(pads_zeroed, PADS_W0)
            nc.scalar.activation(warm[:, :], wpad[0][:, 0, 0, 0:1], ACT.Sqrt)
            gn_sqrt_of(0)
            sc.wait_ge(pads_zeroed, PADS_0)
            halves_x(0)
            gn_sqrt_of(1)
            sc.wait_ge(pads_zeroed, PADS_1)
            sc.wait_ge(params_loaded, 12 * 16)
            sc.wait_ge(evac_scale_ready, 1)
            evacuate(0, 0, 0, 0)
            halves_x(1)
            evacuate(0, 0, 0, 1)
            evacuate(0, 1, 1, 0)
            gn_sqrt(-1, -1)
            halves_x(2)
            evacuate(0, 1, 1, 1)
            normalise_x(3, 3)
            split_hi(0, 3, 3)
            evacuate(0, 2, 2, 0)
            gn_sqrt(1, 1)
            evacuate(0, 2, 2, 1)
            normalise_x(4, 4)
            run_slots(sc, 3, 4, pass1)
            run_slots(sc, 4, NIMG - BODY, pass1)
            run_slots(sc, NIMG - BODY, NIMG, pass1)

            def bn_sqrt(ph):
                sc.wait_ge(bn_var_ready[ph], 1)
                nc.scalar.activation(bn_sd[:, ph:ph + 1], bn_w[:, ph, 3:4], ACT.Sqrt, scale=-1.0).then_inc(bn_sd_ready[ph], 1)

            bn_sqrt(0)
            sc.wait_ge(bn_coef_ready[0], 1)
            sc.wait_ge(evac_scale_ready, 2)

            def pass2(i, r):
                if r + 1 < NIMG and r >= 0:
                    split_hi(1, i + 1, r + 1)
                if r + 2 < NIMG:
                    normalise_y1(i + 2, r + 2)
                if r >= 0:
                    evacuate(1, i, r, 0)
                    evacuate(1, i, r, 1)

            halves_y1()
            run_slots(sc, -1, 2, pass2)
            run_slots(sc, 2, RES - 2, pass2)
            run_slots(sc, RES - 2, NIMG - 2, pass2)
            run_slots(sc, NIMG - 2, NIMG, pass2)
            bn_sqrt(1)
            sc.wait_ge(skip_coef, 3)

            def pass3(q, r):
                if r >= 4:
                    sc.wait_ge(out_stored[r % 4], (q - r % 4) * 8)
                if r >= RES:
                    sc.wait_ge(y2_loaded[r % 4], q * 8 + (32 - 8 * (r % 4) - 8 * RES))
                if r < SPILL:
                    sc.wait_ge(stage_stored[1][r % 2], (q - r % 2) * 32 + (32 * RES + 64))
                if r == 2 or r == 3:
                    sc.wait_ge(stage_stored[1][r % 2], 32 * NIMG)
                base = (q if r < RES else q - RES) * KB
                img = image_of(q, r)
                nc.scalar.activation(ubuf[r % 4], slots_sb[:, bass.ds(base, J), :], ACT.Identity,
                                     bias=skip_b[:, bass.ds(img, 1)], scale=A2).then_inc(u_ready, 1)

            run_slots(sc, 0, BODY, pass3)
            run_slots(sc, BODY, SPILL, pass3)
            run_slots(sc, SPILL, RES, pass3)
            run_slots(sc, RES, NIMG, pass3)

        @block.vector
        def _(dve):
            steps = 0

            def setup_step(ins):
                nonlocal steps
                steps += 1
                ins.then_inc(wprep, 1)
                dve.wait_ge(wprep, steps)

            def weight_absmax(n):
                dve.wait_ge(weights_loaded[n], 32)
                nc.vector.tensor_reduce(wstat[:, n:n + 1], wraw[n][:, :], AX.X, ALU.max,
                                        apply_absolute_value=True).then_inc(absmax_ready, 1)

            def quantise(n):
                dve.wait_ge(absmax_all, n + 1)
                setup_step(nc.vector.tensor_scalar(qscale[:, n:n + 1], wstat[:, n + 2:n + 3], 1.0 / QMAX, None, ALU.mult))
                setup_step(nc.vector.reciprocal(wstat[:, n + 4:n + 5], qscale[:, n:n + 1]))
                setup_step(nc.vector.tensor_scalar(wraw[n][0:C, :], wraw[n][0:C, :], wstat[0:C, n + 4:n + 5], ROUND,
                                                   ALU.mult, ALU.add))
                dve.wait_ge(pads_zeroed, (PADS_W0, PADS)[n])
                nc.vector.tensor_scalar(
                    wpad[n][:, :, 1:4, :].rearrange("o kx ky i -> o i ky kx"),
                    wraw[n][0:C, :].rearrange("o (i ky kx) -> o i ky kx", ky=3, kx=3), ROUND, None,
                    ALU.subtract).then_inc(quantised, 1)
                nc.vector.tensor_scalar(evac_scale[:, n:n + 1], qscale[:, n:n + 1],
                                        1.0 / (GN_SCALE, BN_SCALE)[n], None, ALU.mult).then_inc(evac_scale_ready, 1)

            def power_of_two():
                dve.wait_ge(params_loaded, 12 * 16)
                setup_step(nc.vector.tensor_reduce(pabs[:, 0:1], par[:, 1:3], AX.X, ALU.add, apply_absolute_value=True))
                setup_step(nc.vector.tensor_scalar(pabs[:, 1:2].bitcast(U32), pabs[:, 0:1].bitcast(U32), 0x7F800000, None,
                                                   ALU.bitwise_and))
                setup_step(nc.vector.tensor_scalar(pow2[:, 0:1], pabs[:, 1:2], 2.0 ** -60, None, ALU.max))
                setup_step(nc.vector.reciprocal(pabs[:, 0:1], pow2[:, 0:1]))
                setup_step(nc.vector.tensor_scalar(pow2[:, 1:2], pabs[:, 0:1], BN_SCALE, None, ALU.mult))
                setup_step(nc.vector.tensor_scalar(bn_affine[:, 0, 0:1], par[:, 1:2], 0.5, pow2[:, 1:2], ALU.mult, ALU.mult))
                setup_step(nc.vector.tensor_scalar(bn_affine[:, 0, 1:2], par[:, 2:3], pow2[:, 1:2], None, ALU.mult))
                setup_step(nc.vector.tensor_scalar(bn_affine[:, 1, 0:1], par[:, 4:5], 0.5, None, ALU.mult))
                setup_step(nc.vector.tensor_copy(bn_affine[:, 1, 1:2], par[:, 5:6]))

            def averages():
                dve.wait_ge(masks_made, MASKS)
                pairs = same_channel[:, :].rearrange("p (g e) -> p g e", e=GRP)
                for e in range(GRP):
                    ins = nc.vector.tensor_tensor(gn_avg[:, :].rearrange("p (g e) -> p g e", e=GRP)[:, :, e],
                                                  pairs[:, :, 0], pairs[:, :, 1], ALU.add)
                ins.then_inc(averages_made, 1)

            def bn_average():
                nc.vector.tensor_scalar(bn_avg[:, :], same_channel[:, :], GRP * BODY / NIMG, None,
                                        ALU.mult).then_inc(averages_made, 1)

            def weight_matrices(n):
                dve.wait_ge(transposed, n + 1)
                if n == 0:
                    nc.vector.tensor_copy(wmat[0][:, :, :, :], wt_ps[0][:, :, :, :]).then_inc(wmat_ready, 1)
                else:
                    nc.vector.tensor_scalar(wmat[1][:, :, :, :], wt_ps[1][:, :, :, :], pow2[:, 0:1], None,
                                            ALU.mult).then_inc(wmat_ready, 1)

            def gn_stats(i, r):
                b, m = r % 4, r % 2
                if r == 0:
                    dve.wait_ge(x0_first_rows, 32)
                else:
                    dve.wait_ge(x_loaded[b], i * 8 + (32 - 8 * b))
                if m == 0 and r >= 2:
                    dve.wait_ge(gn_moments, i)
                for t in range(3):
                    if r == 0 and t == 2:
                        dve.wait_ge(x_loaded[b], 32)
                    nc.vector.bn_stats(gn_tup[:, m, t, :], xin[:, b, 1 + t * third:1 + (t + 1) * third, :].rearrange("p k w -> p (k w)"))
                nc.vector.bn_stats(gn_tup[C:P, m, 3, :], xin[C:P, b, 0, :])
                nc.vector.bn_stats(gn_tup[0:C, m, 3, :], xin[0:C, b, J, :]).then_inc(gn_tuples, 1)


            def gn_chain_a(i, r):
                dve.wait_ge(gn_tuples, i + 1)
                if r >= 3:
                    dve.wait_ge(gn_combined, i - 1)
                nc.vector.memset(gn_sq[:, :], 0.0)
                for m in range(2):
                    ins = nc.vector.bn_aggr(gn_mv[:, m, :], gn_tup[:, m].rearrange("p a b -> p (a b)"))
                ins.then_inc(gn_step_a, 1)
                dve.wait_ge(gn_step_a, i - 2)
                nc.vector.tensor_tensor(gn_sq[:, :], gn_mv[:, :, 0], gn_mv[:, :, 0], ALU.mult).then_inc(gn_step_a, 1)
                dve.wait_ge(gn_step_a, i - 1)
                nc.vector.tensor_tensor(gn_mv[:, :, 1], gn_mv[:, :, 1], gn_sq[:, :], ALU.add).then_inc(gn_moments, 2)

            B1_STEPS, B2_STEPS = 3, 7

            def chain(semaphore, base):
                n = 0

                def step(ins):
                    nonlocal n
                    n += 1
                    ins.then_inc(semaphore, 1)
                    dve.wait_ge(semaphore, base + n)
                return step

            def gn_chain_b1(i, r):
                step = chain(gn_step_b, (i - 3) * 5)
                dve.wait_ge(gn_combined, i + 1)
                step(nc.vector.tensor_copy(gn_g[:, :, :].rearrange("p a b -> p (a b)"), stat_ps[:, 0:4]))
                step(nc.vector.tensor_tensor(gn_tmp[:, 0, :], gn_g[:, :, 0], gn_g[:, :, 0], ALU.mult))
                step(nc.vector.tensor_tensor(gn_tmp[:, 1, :], gn_g[:, :, 1], gn_tmp[:, 0, :], ALU.subtract))
                nc.vector.tensor_scalar(gn_var[:, :], gn_tmp[:, 1, :], 0.0, GN_EPS, ALU.max, ALU.add).then_inc(gn_var_ready, 2)

            def gn_chain_b2(i, r):
                step = chain(gn_step_b, (i - 3) * 5 + B1_STEPS)
                dve.wait_ge(gn_sd_ready, i + 1)
                step(nc.vector.reciprocal(gn_tmp[:, 2, :], gn_sd[:, :]))
                step(nc.vector.tensor_tensor(gn_tmp[:, 0, :], gn_tmp[:, 2, :], gn_tmp[:, 2, :], ALU.mult))
                step(nc.vector.tensor_tensor(gn_tmp[:, 1, :], gn_tmp[:, 0, :], gn_var[:, :], ALU.mult))
                step(nc.vector.tensor_scalar(gn_tmp[:, 3, :], gn_tmp[:, 1, :], -0.5 * GN_SCALE, 1.5 * GN_SCALE, ALU.mult, ALU.add))
                if r >= 3:
                    dve.wait_ge(act_ready[0], i - 1)
                step(nc.vector.tensor_tensor(gn_s[:, :], gn_tmp[:, 3, :], gn_tmp[:, 2, :], ALU.mult))
                nc.vector.scalar_tensor_tensor(out=gn_b[:, :], in0=gn_g[:, :, 0], scalar=-1.0, in1=gn_s[:, :],
                                               op0=ALU.mult, op1=ALU.mult).then_inc(gn_coef_ready, 2)
                step(nc.vector.tensor_copy(gn_s_all[:, bass.ds(i - 1, 2)], gn_s[:, :]))
                dve.wait_ge(gn_coef_ready, i + 1)
                step(nc.vector.tensor_copy(gn_b_all[:, bass.ds(i - 1, 2)], gn_b[:, :]))

            def gn_first_a(m):
                mean, second = gn_mv[:, m, 0:1], gn_mv[:, m, 1:2]
                dve.wait_ge(gn_tuples, m + 1)
                nc.vector.memset(gn_sq[:, m:m + 1], 0.0)
                setup_step(nc.vector.bn_aggr(gn_mv[:, m, :], gn_tup[:, m].rearrange("p a b -> p (a b)")))
                nc.vector.scalar_tensor_tensor(out=second, in0=mean, scalar=mean, in1=second,
                                               op0=ALU.mult, op1=ALU.add).then_inc(gn_moments, 1)

            def gn_first_b1(m):
                mean = gn_g[:, m, 0:1]
                dve.wait_ge(gn_combined, m + 1)
                setup_step(nc.vector.tensor_copy(gn_g[:, m, :], stat_ps[:, 2 * m:2 * m + 2]))
                setup_step(nc.vector.scalar_tensor_tensor(out=gn_tmp[:, 0, m:m + 1], in0=mean, scalar=mean,
                                                          in1=gn_g[:, m, 1:2], op0=ALU.mult, op1=ALU.subtract))
                nc.vector.tensor_scalar(gn_var[:, m:m + 1], gn_tmp[:, 0, m:m + 1], 0.0, GN_EPS, ALU.min,
                                        ALU.subtract).then_inc(gn_var_ready, 1)

            def gn_first_b2(m):
                root, correction, scale = gn_tmp[:, 2, m:m + 1], gn_tmp[:, 1, m:m + 1], gn_s[:, m:m + 1]
                dve.wait_ge(gn_sd_ready, m + 1)
                setup_step(nc.vector.reciprocal(root, gn_sd[:, m:m + 1]))
                setup_step(nc.vector.scalar_tensor_tensor(out=correction, in0=root, scalar=root, in1=gn_var[:, m:m + 1],
                                                          op0=ALU.mult, op1=ALU.mult))
                setup_step(nc.vector.tensor_scalar(gn_tmp[:, 3, m:m + 1], correction, 0.5 * GN_SCALE, 1.5 * GN_SCALE,
                                                   ALU.mult, ALU.add))
                setup_step(nc.vector.tensor_tensor(scale, gn_tmp[:, 3, m:m + 1], root, ALU.mult))
                nc.vector.scalar_tensor_tensor(out=gn_b[:, m:m + 1], in0=gn_g[:, m, 0:1], scalar=-1.0, in1=scale,
                                               op0=ALU.mult, op1=ALU.mult).then_inc(gn_coef_ready, 1)
                dve.wait_ge(gn_coef_ready, m + 1)
                nc.vector.tensor_copy(gn_s_all[:, m:m + 1], scale)
                nc.vector.tensor_copy(gn_b_all[:, m:m + 1], gn_b[:, m:m + 1])

            def half_lo_x(i):
                k, m = i % 2, i % 2
                for a, b, k0, k1 in ((C, P, 0, 1), (0, P, 1, HALF)):
                    ins = nc.vector.tensor_scalar(act[a:b, k, k0:k1, :], xin[a:b, i % 4, k0:k1, :], gn_s[a:b, m:m + 1],
                                                  gn_b[a:b, m:m + 1], ALU.mult, ALU.add)
                ins.then_inc(half_act[0], 1)
                dve.wait_ge(half_act[0], i + 1)
                dve.wait_ge(half_hi[0], i + 1)
                nc.vector.tensor_tensor(lo[:, k, 0:HALF, 1:1 + W], act[:, k, 0:HALF], hi[:, k, 0:HALF, 1:1 + W],
                                        ALU.subtract).then_inc(half_lo[0], 1)

            def half_lo_y1():
                for a, b, k0, k1 in ((C, P, 0, 1), (0, P, 1, HALF)):
                    ins = nc.vector.tensor_scalar(act[a:b, 0, k0:k1, :], slots_sb[a:b, k0:k1, :], A1[a:b, :], B1[a:b, :],
                                                  ALU.mult, ALU.add)
                ins.then_inc(half_act[1], 1)
                dve.wait_ge(half_act[1], 1)
                dve.wait_ge(half_hi[1], 1)
                nc.vector.scalar_tensor_tensor(out=lo[:, 0, 0:HALF, 1:1 + W], in0=act[:, 0, 0:HALF], scalar=0.0,
                                               in1=hi[:, 0, 0:HALF, 1:1 + W], op0=ALU.max,
                                               op1=ALU.subtract).then_inc(half_lo[1], 1)

            def rest_lo(ph, i):
                dve.wait_ge(hi_ready[ph], i + 1)
                nc.vector.tensor_tensor(lo[:, i % 2, HALF:KB, 1:1 + W], act[:, i % 2, HALF:KB], hi[:, i % 2, HALF:KB, 1:1 + W],
                                        ALU.subtract).then_inc(lo_ready[ph], 1)

            def split_lo(ph, i, r):
                k = r % 2
                dve.wait_ge(hi_ready[ph], i + 1)
                nc.vector.tensor_tensor(lo[:, k, :, 1:1 + W], act[:, k], hi[:, k, :, 1:1 + W], ALU.subtract).then_inc(lo_ready[ph], 1)

            def bn_stats(ph, i, r, p):
                dve.wait_ge(pair_evac[ph][p], i + 1)
                if r % BODY == 0 and p == 0 and r >= BODY:
                    dve.wait_ge(bn_sums[ph], i)
                rows = ROWS_PER_BANK
                for c in range(2 * p, 2 * p + 2):
                    ins = nc.vector.bn_stats(bn_tup[:, (r % BODY) * NCH + c, :],
                                             stage[:, r % 2, c * rows:(c + 1) * rows, :].rearrange("q j w -> q (j w)"))
                if p == NPAIR - 1:
                    ins.then_inc(stage_read[ph], 1)

            def bn_accumulate(ph, i, r):
                base = i - (BODY - 1)
                mean, second = bn_mv[:, 0:1], bn_mv[:, 1:2]
                dve.wait_ge(stage_read[ph], i + 1)
                nc.vector.memset(bn_sq[:, :], 0.0)
                nc.vector.bn_aggr(bn_mv[:, :], bn_tup[:, :, :].rearrange("p a b -> p (a b)")).then_inc(bn_step[ph], BODY // 2)
                dve.wait_ge(bn_step[ph], base + BODY // 2)
                nc.vector.scalar_tensor_tensor(out=second, in0=mean, scalar=mean, in1=second, op0=ALU.mult,
                                               op1=ALU.add).then_inc(bn_step[ph], BODY // 2)
                dve.wait_ge(bn_step[ph], base + BODY)
                nc.vector.tensor_tensor(bn_acc[ph][:, :], bn_acc[ph][:, :], bn_mv[:, :], ALU.add).then_inc(bn_sums[ph], BODY)

            def bn_coefficients(ph):
                step = chain(bn_chain[ph], 0)
                v = lambda c: bn_w[:, ph, c:c + 1]
                mean, neg_mean, neg_var, root = v(0), v(4), v(3), v(5)
                half_gamma, beta = bn_affine[:, ph, 0:1], bn_affine[:, ph, 1:2]
                dve.wait_ge(bn_combined[ph], 1)
                step(nc.vector.tensor_copy(bn_w[:, ph, 0:2], stat_ps[:, 0:2]))
                step(nc.vector.scalar_tensor_tensor(out=v(2), in0=mean, scalar=mean, in1=v(1), op0=ALU.mult, op1=ALU.subtract))
                nc.vector.tensor_scalar(neg_var, v(2), 0.0, BN_EPS, ALU.min, ALU.subtract).then_inc(bn_var_ready[ph], 1)
                step(nc.vector.tensor_scalar(neg_mean, mean, -1.0, None, ALU.mult))
                dve.wait_ge(bn_sd_ready[ph], 1)
                step(nc.vector.reciprocal(root, bn_sd[:, ph:ph + 1]))
                nc.vector.tensor_tensor(v(7), root, half_gamma, ALU.mult)
                step(nc.vector.scalar_tensor_tensor(out=v(6), in0=root, scalar=root, in1=neg_var, op0=ALU.mult, op1=ALU.mult))
                step(nc.vector.scalar_tensor_tensor(out=v(8), in0=v(6), scalar=3.0, in1=v(7), op0=ALU.add, op1=ALU.mult))
                shift = nc.vector.scalar_tensor_tensor(out=v(9), in0=v(8), scalar=neg_mean, in1=beta, op0=ALU.mult, op1=ALU.add)
                if ph == 0:
                    shift.then_inc(bn_coef_ready[0], 1)
                else:
                    step(shift)
                    nc.vector.tensor_scalar(skip_b[:, :], gn_b_all[:, :], v(9), None, ALU.add).then_inc(skip_coef, 1)

            def skip_coefficients():
                nc.vector.tensor_scalar(skip_s[:, :], gn_s_all[:, :], 1.0 / GN_SCALE, None, ALU.mult).then_inc(skip_coef, 1)
                nc.vector.tensor_scalar(gn_b_all[:, :], gn_b_all[:, :], 1.0 / GN_SCALE, None, ALU.mult).then_inc(skip_coef, 1)
                dve.wait_ge(skip_coef, 2)

            def lo_and_last_bn(ph, i, r):
                if r >= 1:
                    bn_stats(ph, i - 1, r - 1, 1)
                if 0 <= r + 1 < NIMG:
                    split_lo(ph, i + 1, r + 1)
                if r >= 1 and r % BODY == 0:
                    bn_accumulate(ph, i - 1, r - 1)

            def pass1(i, r):
                pair_complete = r % 2 == 1 and r + 4 < NIMG
                if r + 4 < NIMG:
                    gn_stats(i + 4, r + 4)
                if pair_complete:
                    gn_chain_a(i + 4, r + 4)
                lo_and_last_bn(0, i, r)
                if pair_complete:
                    gn_chain_b1(i + 4, r + 4)
                if r < NIMG:
                    bn_stats(0, i, r, 0)
                if pair_complete:
                    gn_chain_b2(i + 4, r + 4)

            weight_absmax(0)
            for n in range(2):
                setup_step(nc.vector.memset(bn_acc[n][:, :], 0.0))
            quantise(0)
            averages()
            weight_matrices(0)
            gn_stats(0, 0)
            gn_first_a(0)
            gn_first_b1(0)
            gn_first_b2(0)
            dve.wait_ge(pads_zeroed, PADS_1)
            half_lo_x(0)
            gn_stats(1, 1)
            gn_first_a(1)
            rest_lo(0, 0)
            gn_first_b1(1)
            gn_first_b2(1)
            half_lo_x(1)
            gn_stats(2, 2)
            rest_lo(0, 1)
            gn_stats(3, 3)
            gn_chain_a(3, 3)
            gn_chain_b1(3, 3)
            gn_chain_b2(3, 3)
            half_lo_x(2)
            bn_stats(0, 0, 0, 0)
            bn_stats(0, 0, 0, 1)
            rest_lo(0, 2)
            gn_stats(4, 4)
            bn_stats(0, 1, 1, 0)
            gn_stats(5, 5)
            gn_chain_a(5, 5)
            split_lo(0, 3, 3)
            gn_chain_b1(5, 5)
            bn_stats(0, 1, 1, 1)
            gn_chain_b2(5, 5)
            bn_stats(0, 2, 2, 0)
            gn_stats(6, 6)
            run_slots(dve, 3, BODY, pass1)
            run_slots(dve, BODY, NIMG - BODY, pass1)
            bn_average()
            weight_absmax(1)
            power_of_two()
            run_slots(dve, NIMG - BODY, NIMG - BODY + 1, pass1)
            quantise(1)
            run_slots(dve, NIMG - BODY + 1, NIMG - 1, pass1)
            weight_matrices(1)
            run_slots(dve, NIMG - 1, NIMG + 1, pass1)
            bn_coefficients(0)

            def pass2(i, r):
                lo_and_last_bn(1, i, r)
                if 0 <= r < NIMG:
                    bn_stats(1, i, r, 0)

            dve.wait_ge(bn_coef_ready[0], 1)
            half_lo_y1()
            rest_lo(1, 0)
            run_slots(dve, 0, BODY, pass2)
            run_slots(dve, BODY, NIMG - BODY, pass2)
            skip_coefficients()
            run_slots(dve, NIMG - BODY, NIMG + 1, pass2)
            bn_coefficients(1)

            def pass3(q, r):
                img = image_of(q, r)
                u, xs = ubuf[r % 4], xin[:, r % 4, 0:J, :]
                dve.wait_ge(x3_loaded[r % 4], q * 8 + (32 - 8 * (r % 4)))
                dve.wait_ge(u_ready, q + 1)
                nc.vector.scalar_tensor_tensor(out=u, in0=xs, scalar=skip_s[:, bass.ds(img, 1)], in1=u,
                                               op0=ALU.mult, op1=ALU.add).then_inc(sum_ready, 1)
                dve.wait_ge(sum_ready, q + 1)
                nc.vector.scalar_tensor_tensor(out=u, in0=u, scalar=0.0, in1=xs,
                                               op0=ALU.max, op1=ALU.add).then_inc(out_ready, 1)

            run_slots(dve, 0, SPILL, pass3)
            run_slots(dve, SPILL, RES, pass3)
            run_slots(dve, RES, NIMG, pass3)

        @block.tensor
        def _(pe):
            pe.wait_ge(masks_made, 1)

            def weight_transposes(n):
                pe.wait_ge(quantised, n + 1)
                for kx in range(3):
                    for pair, o, ky in ((0, 0, 1), (0, 1, 0), (1, 0, 3), (1, 1, 2)):
                        mm = nc.tensor.transpose(wt_ps[n][:, kx, pair, o * C:(o + 1) * C],
                                                 wpad[n][:, kx, ky:ky + 2, :].rearrange("o a i -> o (a i)"), ident[:, :])
                mm.then_inc(transposed, 1)

            weight_transposes(0)

            def gn_combine(i, r):
                pe.wait_ge(gn_moments, i + 1)
                if r >= 3:
                    pe.wait_ge(gn_var_ready, i - 1)
                nc.tensor.matmul(stat_ps[:, 0:4], gn_avg[:, :], gn_mv[:, :, :].rearrange("p a b -> p (a b)"),
                                 start=True, stop=True).then_inc(gn_combined, 2)

            def conv(ph, i, r, between=None, at=(0, 2)):
                k = r % 2
                halves = r < DIRECT[ph]
                for p in range(NPAIR):
                    if halves and p == 0:
                        pe.wait_ge(half_lo[ph], i + 1)
                    elif halves or p == 0:
                        pe.wait_ge(hi_ready[ph], i + 1)
                        pe.wait_ge(lo_ready[ph], i + 1)
                    if r >= 1:
                        pe.wait_ge(pair_evac[ph][p], i)
                    for kx in range(3):
                        for pair in range(2):
                            for part in (hi, lo):
                                for c in range(2 * p, 2 * p + 2):
                                    k0 = c * ROWS_PER_BANK + pair
                                    first = kx == 0 and pair == 0 and part is hi
                                    last = kx == 2 and pair == 1 and part is lo
                                    mm = nc.tensor.matmul(conv_ps[:, c, 0:CH], wmat[ph][:, kx, pair, :],
                                                          part[:, k, k0:k0 + ROWS_PER_BANK, kx:kx + W],
                                                          start=first, stop=last)
                        if kx == 2:
                            mm.then_inc(pair_done[ph][p], 1)
                        if between and (p, kx) == at:
                            between()

            def gn_combine_of(m):
                pe.wait_ge(gn_moments, m + 1)
                nc.tensor.matmul(stat_ps[:, 2 * m:2 * m + 2], gn_avg[:, :], gn_mv[:, m, :],
                                 start=True, stop=True).then_inc(gn_combined, 1)

            def pass1(i, r):
                if r % 2 == 1 and r + 4 < NIMG:
                    conv(0, i, r, lambda: gn_combine(i + 4, r + 4))
                else:
                    conv(0, i, r)

            pe.wait_ge(averages_made, 1)
            gn_combine_of(0)
            pe.wait_ge(wmat_ready, 1)
            conv(0, 0, 0, lambda: gn_combine_of(1), at=(0, 1))
            conv(0, 1, 1, lambda: gn_combine(3, 3), at=(1, 0))
            conv(0, 2, 2, lambda: gn_combine(5, 5), at=(1, 2))
            run_slots(pe, 3, BODY, pass1)
            run_slots(pe, BODY, NIMG - BODY, pass1)
            run_slots(pe, NIMG - BODY, NIMG - 2, pass1)
            weight_transposes(1)
            run_slots(pe, NIMG - 2, NIMG, pass1)

            def bn_combine(ph):
                pe.wait_ge(averages_made, 2)
                pe.wait_ge(bn_sums[ph], NIMG)
                nc.tensor.matmul(stat_ps[:, 0:2], bn_avg[:, :], bn_acc[ph][:, :], start=True, stop=True).then_inc(bn_combined[ph], 1)

            bn_combine(0)
            pe.wait_ge(wmat_ready, 2)
            run_slots(pe, 0, BODY, lambda i, r: conv(1, i, r))
            run_slots(pe, BODY, NIMG, lambda i, r: conv(1, i, r))
            bn_combine(1)


_INS = ['x', 'L0_conv_w1', 'L0_conv_b1', 'L0_conv_gamma1', 'L0_conv_beta1',
        'L0_conv_w2', 'L0_conv_b2', 'L0_conv_gamma2', 'L0_conv_beta2']


def kernel(**inputs):
    import numpy as _np
    import concourse.bacc as _bacc
    from concourse import mybir as _mybir
    from concourse.bass_utils import run_bass_kernel_spmd as _run

    nc = _bacc.Bacc("TRN2", target_bir_lowering=False, num_devices=1)
    arrays, args = {}, []
    for name in _INS:
        a = _np.ascontiguousarray(inputs[name])
        arrays[f"in_{name}_dram"] = a
        args.append(nc.dram_tensor(f"in_{name}_dram", a.shape, _mybir.dt.from_np(a.dtype), kind="ExternalInput").ap())
    shape = inputs["x"].shape
    args.append(nc.dram_tensor("out_0_dram", shape, _mybir.dt.float32, kind="ExternalOutput").ap())
    conv_block_kernel(nc, *args)
    r = _run(nc, [arrays], core_ids=[0])
    return r.results[0]["out_0_dram"]
```

```python
from contextlib import ExitStack

import concourse.bass as bass
from concourse import mybir

F32 = mybir.dt.float32
F16 = mybir.dt.float16
BF16 = mybir.dt.bfloat16
U32 = mybir.dt.uint32
ALU = mybir.AluOpType
ACT = mybir.ActivationFunctionType
AX = mybir.AxisListType

P = 128
BODY = 4
GN_EPS = 1e-5
BN_EPS = 1e-5
QMAX = 127.0
ROUND = 12582912.0
GN_SCALE = 512.0
BN_SCALE = 64.0


def conv_block_kernel(nc, x, w1, b1, g1, be1, w2, b2, g2, be2, out):
    NIMG, C, H, W = x.shape
    assert C == 64 and H % 2 == 0
    J = H // 2
    KB = J + 1
    PIX = J * W
    ROWS_PER_BANK = 7
    NCH = J // ROWS_PER_BANK
    CH = ROWS_PER_BANK * W
    NPAIR = NCH // 2
    HALF = 2 * ROWS_PER_BANK + 1
    DIRECT = (3, 1)
    assert NPAIR == 2 and J % (2 * ROWS_PER_BANK) == 0 and NIMG % BODY == 0 and CH <= 512
    RES = 20
    SPILL = NIMG - RES
    assert RES % BODY == 0 and SPILL % BODY == 0 and SPILL <= RES - 2 * BODY + BODY
    GRP = 2

    with ExitStack() as ctx:
        def sb(name, shape, dt):
            return ctx.enter_context(nc.sbuf_tensor(name, shape, dt))

        def psum(name, shape, dt):
            return ctx.enter_context(nc.psum_tensor(name, shape, dt))

        def sem(name):
            return ctx.enter_context(nc.semaphore(name))

        y1_spill = nc.dram_tensor("y1_spill", [SPILL, P, PIX], F32, kind="Internal").ap()
        y2_spill = nc.dram_tensor("y2_spill", [SPILL, C, H, W], F32, kind="Internal").ap()

        slots_sb = sb("slots_sb", [P, RES * J + 2, W], F32)
        xin = sb("xin", [P, 4 * J + 1, W], F32)
        act = sb("act", [P, 2, KB, W], F32)
        spare = sb("spare", [P, PIX], F32)
        spare2 = sb("spare2", [P, PIX], F32)
        split = sb("split", [P, 2, 2, KB, W], F16)
        hi, lo = split[:, 0], split[:, 1]
        stage = sb("stage", [P, 2, J, W], F32)
        first_only = sb("first_only", [P, PIX], F32)
        cuts = [0, C * 9, C * 9 + 15 * C // 2, C * 9 + 15 * C // 2 + 3 * P, C * 9 + 15 * C // 2 + 4 * P]
        assert cuts[-1] <= PIX
        part = lambda n: first_only[:, cuts[n]:cuts[n + 1]]
        wraw = part(0)
        wpad = part(1).bitcast(BF16)[0:C].rearrange("o (x y i) -> o x y i", x=3, y=5)
        wmat = [part(2).bitcast(BF16).rearrange("p (x r m) -> p x r m", x=3, r=2), sb("wmat2", [P, 3, 2, P], BF16)]
        same_channel = part(3)
        gn_avg = spare2[:, 0:P]
        ident = spare2[0:C, P:P + C // 2].bitcast(BF16)
        bn_avg = sb("bn_avg", [P, P], F32)
        par = sb("par", [P, 6], F32)
        wstat = sb("wstat", [P, 8], F32)
        qscale = sb("qscale", [P, 2], F32)
        evac_scale = sb("evac_scale", [P, 2], F32)
        pow2 = sb("pow2", [P, 2], F32)
        pabs = sb("pabs", [P, 2], F32)
        warm = sb("warm", [C, 1], F32)
        gn_tup = sb("gn_tup", [P, 2, 4, 6], F32)
        gn_mv = sb("gn_mv", [P, 2, 2], F32)
        gn_sq = sb("gn_sq", [P, 2], F32)
        gn_g = sb("gn_g", [P, 2, 2], F32)
        gn_var = sb("gn_var", [P, 2], F32)
        gn_sd = sb("gn_sd", [P, 2], F32)
        gn_tmp = sb("gn_tmp", [P, 4, 2], F32)
        gn_s = sb("gn_s", [P, 2], F32)
        gn_b = sb("gn_b", [P, 2], F32)
        gn_s_all = sb("gn_s_all", [P, NIMG], F32)
        gn_b_all = sb("gn_b_all", [P, NIMG], F32)
        skip_s = sb("skip_s", [P, NIMG], F32)
        skip_b = sb("skip_b", [P, NIMG], F32)
        bn_tup = sb("bn_tup", [P, BODY * NCH, 6], F32)
        bn_mv = sb("bn_mv", [P, 2], F32)
        bn_sq = sb("bn_sq", [P, 1], F32)
        bn_acc = [sb(f"bn_acc{n}", [P, 2], F32) for n in (1, 2)]
        bn_w = sb("bn_w", [P, 2, 10], F32)
        bn_affine = sb("bn_affine", [P, 2, 2], F32)
        bn_sd = sb("bn_sd", [P, 2], F32)

        conv_ps = psum("conv_ps", [P, 4, 512], F32)
        stat_ps = psum("stat_ps", [P, 512], F32)
        wt_ps = [psum(f"wt_ps{n}", [P, 3, 2, P], BF16) for n in (1, 2)]

        params_loaded = sem("params_loaded")
        weights_loaded = [sem(f"weights_loaded{n}") for n in (1, 2)]
        masks_zeroed = sem("masks_zeroed")
        masks_made = sem("masks_made")
        pads_zeroed = sem("pads_zeroed")
        wprep = sem("wprep")
        absmax_ready = sem("absmax_ready")
        absmax_all = sem("absmax_all")
        quantised = sem("quantised")
        transposed = sem("transposed")
        wmat_ready = sem("wmat_ready")
        evac_scale_ready = sem("evac_scale_ready")
        averages_made = sem("averages_made")
        x0_first_rows = sem("x0_first_rows")
        x_loaded = [sem(f"x_loaded{b}") for b in range(4)]
        gn_tuples = sem("gn_tuples")
        gn_step_a = sem("gn_step_a")
        gn_moments = sem("gn_moments")
        gn_combined = sem("gn_combined")
        gn_step_b = sem("gn_step_b")
        gn_copied = sem("gn_copied")
        gn_var_ready = sem("gn_var_ready")
        gn_sd_ready = sem("gn_sd_ready")
        gn_coef_ready = sem("gn_coef_ready")
        half_act = [sem(f"half_act{n}") for n in (1, 2)]
        half_hi = [sem(f"half_hi{n}") for n in (1, 2)]
        half_lo = [sem(f"half_lo{n}") for n in (1, 2)]
        act_ready = [sem(f"act_ready{n}") for n in (1, 2)]
        hi_ready = [sem(f"hi_ready{n}") for n in (1, 2)]
        lo_ready = [sem(f"lo_ready{n}") for n in (1, 2)]
        pair_done = [[sem(f"pair_done{n}_{p}") for p in range(2)] for n in (1, 2)]
        pair_evac = [[sem(f"pair_evac{n}_{p}") for p in range(2)] for n in (1, 2)]
        stage_read = [sem(f"stage_read{n}") for n in (1, 2)]
        stage_stored = [[sem(f"stage_stored{n}_{b}") for b in range(2)] for n in (1, 2)]
        bn_tuples = [sem(f"bn_tuples{n}") for n in (1, 2)]
        bn_step = [sem(f"bn_step{n}") for n in (1, 2)]
        bn_sums = [sem(f"bn_sums{n}") for n in (1, 2)]
        bn_combined = [sem(f"bn_combined{n}") for n in (1, 2)]
        bn_chain = [sem(f"bn_chain{n}") for n in (1, 2)]
        bn_var_ready = [sem(f"bn_var_ready{n}") for n in (1, 2)]
        bn_sd_ready = [sem(f"bn_sd_ready{n}") for n in (1, 2)]
        bn_coef_ready = [sem(f"bn_coef_ready{n}") for n in (1, 2)]
        y1_loaded = [sem(f"y1_loaded{b}") for b in range(4)]
        skip_coef = sem("skip_coef")
        x3_own_loaded = [sem(f"x3_own_loaded{q}") for q in range(13)]
        x3_loaded = [sem(f"x3_loaded{b}") for b in range(4)]
        y2_loaded = [sem(f"y2_loaded{b}") for b in range(4)]
        u_ready = sem("u_ready")
        sum_ready = sem("sum_ready")
        out_ready = sem("out_ready")
        out_stored = [sem(f"out_stored{b}") for b in range(4)]

        A1, B1, A2, B2 = (bn_w[:, n, c:c + 1] for n in (0, 1) for c in (8, 9))

        def odd_even(ap):
            return ap.rearrange("c (j h) w -> h c j w", h=2)

        def run_slots(eng, start, stop, body):
            n = (stop - start) // BODY
            if n >= 2 and (stop - start) % BODY == 0:
                with eng.Fori(0, n) as it:
                    for k in range(BODY):
                        body(it * BODY + (start + k), start + k)
            else:
                for i in range(start, stop):
                    body(i, i)

        def slot_row(slot, r):
            return slot * J + (1 if r >= SPILL else 0)

        def xin_rows(b, k0, k1):
            return slice(b * J + k0, b * J + k1)

        def image_of(q, r):
            return q if r < SPILL else q + SPILL if r < RES else q - RES + SPILL

        third = (J - 1) // 3
        cut = 1 + 2 * third

        flat = lambda ap: ap.rearrange("p k w -> p (k w)")[:, 0:PIX]
        split_f32 = split[:, :, :, :, :].rearrange("p a b k w -> p (a b k w)").bitcast(F32)
        own_buffers = [flat(xin[:, xin_rows(b, 0, J)]) for b in range(4)] + [
            spare[:, :], spare2[:, :], first_only[:, :], flat(act[:, 0]), flat(act[:, 1]), flat(stage[:, 0]),
            split_f32[:, 0:PIX], split_f32[:, PIX:2 * PIX], flat(stage[:, 1])]
        EARLY = 7
        OWN = len(own_buffers)

        def first_use(b):
            return OWN + (b - OWN) % 4

        def x3_buffer(r):
            return own_buffers[r if r < OWN else r % 4]


        PADS_W, PADS_0, PADS_1 = 1, 4, 7
        MASKS = 4
        WARM0, WARM1, WARM2, WARM3 = 8, 12, 8, 20

        block = ctx.enter_context(nc.Block())

        @block.sync
        def _(sp):
            def load_x(j, r):
                b = r % 4
                if r >= 4:
                    sp.wait_ge(act_ready[0], j - 3)
                    if r - 4 < DIRECT[0]:
                        sp.wait_ge(half_lo[0], j - 3)
                src = odd_even(x[j])
                if r == 0:
                    sp.dma_start(xin[0:C, 1:cut, :], src[1][:, 0:cut - 1, :]).then_inc(x0_first_rows, 16)
                    sp.dma_start(xin[C:P, 0:cut, :], src[0][:, 0:cut, :]).then_inc(x0_first_rows, 16)
                    sp.dma_start(xin[0:C, cut:KB, :], src[1][:, cut - 1:J, :]).then_inc(x_loaded[b], 16)
                    sp.dma_start(xin[C:P, cut:J, :], src[0][:, cut:J, :]).then_inc(x_loaded[b], 16)
                    return
                sp.dma_start(xin[0:C, xin_rows(b, 1, KB), :], src[1]).then_inc(x_loaded[b], 16)
                sp.dma_start(xin[C:P, xin_rows(b, 0, J), :], src[0]).then_inc(x_loaded[b], 16)

            for h in range(2):
                sp.dma_start(wraw[C * h:C * h + C, :], w1.rearrange("o i a b -> o (i a b)")).then_inc(weights_loaded[0], 16)
            for j in range(3):
                load_x(j, j)
            for col, v in enumerate((b1, g1, be1, b2, g2, be2)):
                for h in range(2):
                    sp.dma_start(par[C * h:C * h + C, col:col + 1], v.rearrange("(c a) -> c a", a=1)).then_inc(params_loaded, 16)
            for j in range(3, 6):
                load_x(j, j)
            sp.wait_ge(quantised, 1)
            for h in range(2):
                sp.dma_start(wraw[C * h:C * h + C, :], w2.rearrange("o i a b -> o (i a b)")).then_inc(weights_loaded[1], 16)

            def pass1(i, r):
                if r + 6 < NIMG:
                    load_x(i + 6, r + 6)
                b = r % 2
                sp.wait_ge(pair_evac[0][1], i + 1)
                done = stage_stored[0][b]
                if r < SPILL:
                    for h in range(2):
                        sp.dma_start(y1_spill[i, C * h:C * h + C, :],
                                     stage[C * h:C * h + C, b].rearrange("p j w -> p (j w)")).then_inc(done, 16)
                else:
                    base = slot_row(i - SPILL, r - SPILL)
                    sp.dma_start(slots_sb[0:C, bass.ds(base + 1, J), :], stage[C:P, b]).then_inc(done, 16)
                    sp.dma_start(slots_sb[C:P, bass.ds(base, J), :], stage[0:C, b]).then_inc(done, 16)

            run_slots(sp, 0, BODY, pass1)
            run_slots(sp, BODY, SPILL, pass1)
            run_slots(sp, SPILL, NIMG - 2 * BODY, pass1)
            run_slots(sp, NIMG - 2 * BODY, NIMG - BODY, pass1)
            run_slots(sp, NIMG - BODY, NIMG, pass1)
            for b in range(2):
                sp.wait_ge(stage_stored[0][b], 16 * NIMG)

            def load_y1(p, r):
                b = r % 4
                base = slot_row(p - RES, r - RES)
                img = p - RES
                sp.dma_start(slots_sb[0:C, bass.ds(base + 1, J), :],
                             y1_spill[img, C:P, :].rearrange("p (j w) -> p j w", w=W)).then_inc(y1_loaded[b], 16)
                sp.dma_start(slots_sb[C:P, bass.ds(base, J), :],
                             y1_spill[img, 0:C, :].rearrange("p (j w) -> p j w", w=W)).then_inc(y1_loaded[b], 16)

            def load_x3(q, r, img):
                if r >= OWN + 4:
                    sp.wait_ge(out_ready, q - 3)
                elif r >= OWN:
                    sp.wait_ge(out_ready, r % 4 + 1)
                buf = x3_buffer(r).rearrange("p (j w) -> p j w", w=W)
                loaded = x3_own_loaded[r] if r < OWN else x3_loaded[r % 4]
                src = x[img].rearrange("c (h r) w -> h c r w", h=2)
                for h in range(2):
                    sp.dma_start(buf[C * h:C * h + C], src[h]).then_inc(loaded, 16)

            def pass2(i, r):
                if RES <= r + 4 < NIMG:
                    sp.wait_ge(act_ready[1], i + 1)
                    load_y1(i + 4, r + 4)
                if RES - 4 - 8 <= r < RES - 4 - 8 + EARLY:
                    load_x3(r - 8, r - 8, r - 8)
                b = r % 2
                sp.wait_ge(pair_evac[1][1], i + 1)
                done = stage_stored[1][b]
                if r < SPILL:
                    dst = odd_even(y2_spill[i])
                    for h in range(2):
                        for part in range(2):
                            sp.dma_start(dst[h][:, part * J // 2:(part + 1) * J // 2, :],
                                         stage[C * h:C * h + C, b, part * J // 2:(part + 1) * J // 2]).then_inc(done, 16)
                else:
                    base = slot_row(i if r < RES else i - RES, r % RES)
                    for h in range(2):
                        for part in range(2):
                            sp.dma_start(
                                slots_sb[C * part:C * part + C, bass.ds(base + h, J // 2, 2), :],
                                stage[C * h:C * h + C, b, part * J // 2:(part + 1) * J // 2]).then_inc(done, 16)

            run_slots(sp, 0, SPILL - BODY, pass2)
            run_slots(sp, SPILL - BODY, SPILL, pass2)
            run_slots(sp, SPILL, RES - BODY, pass2)
            run_slots(sp, RES - BODY, RES, pass2)
            run_slots(sp, RES, NIMG - BODY, pass2)
            run_slots(sp, NIMG - BODY, NIMG - 2, pass2)
            sp.wait_ge(lo_ready[1], NIMG - 1)
            load_x3(EARLY, EARLY, EARLY)
            run_slots(sp, NIMG - 2, NIMG - 1, pass2)
            sp.wait_ge(lo_ready[1], NIMG)
            load_x3(EARLY + 1, EARLY + 1, EARLY + 1)
            sp.wait_ge(stage_stored[1][0], 32 * NIMG)
            sp.wait_ge(stage_read[1], NIMG - 1)
            load_x3(EARLY + 2, EARLY + 2, EARLY + 2)
            run_slots(sp, NIMG - 1, NIMG, pass2)
            for q in (EARLY + 3, EARLY + 4):
                sp.wait_ge(pair_done[1][1], NIMG)
                load_x3(q, q, q)
            sp.wait_ge(stage_read[1], NIMG)
            sp.wait_ge(stage_stored[1][1], 32 * NIMG)
            load_x3(OWN - 1, OWN - 1, image_of(OWN - 1, OWN - 1))
            for b in range(2):
                sp.wait_ge(stage_stored[1][b], 32 * NIMG)

            def load_y2(m, r):
                sp.wait_ge(out_stored[r % 4], (m - r % 4) * 8 + 32)
                for h in range(2):
                    sp.dma_start(slots_sb[C * h:C * h + C, bass.ds(slot_row(m, r), J), :],
                                 y2_spill[m].rearrange("c (h r) w -> h c r w", h=2)[h]).then_inc(y2_loaded[r % 4], 16)

            def pass3(q, r):
                sp.wait_ge(out_ready, q + 1)
                dst = out[image_of(q, r)].rearrange("c (h r) w -> h c r w", h=2)
                base = slot_row(q if r < RES else q - RES, r % RES)
                for h in range(2):
                    sp.dma_start(dst[h], slots_sb[C * h:C * h + C, bass.ds(base, J), :]).then_inc(out_stored[r % 4], 16)
                if r < 4:
                    n = first_use(q)
                    load_x3(n, n, image_of(n, n))
                elif OWN <= r < NIMG - 4:
                    load_x3(q + 4, r + 4, image_of(q + 4, r + 4))
                if 2 <= r < SPILL + 2:
                    load_y2(q - 2, r - 2)

            for start, stop in ((0, SPILL), (SPILL, RES - 4), (RES - 4, RES), (RES, NIMG - 4), (NIMG - 4, NIMG)):
                for first in ([start] if start else [0, 4, 8]):
                    run_slots(sp, first, stop if start else first + 4, pass3)
            for b in range(4):
                sp.wait_ge(out_stored[b], 8 * NIMG)

        @block.gpsimd
        def _(pool):
            nc.gpsimd.memset(ident[:, :], 0.0).then_inc(masks_zeroed, 1)
            nc.gpsimd.memset(same_channel[:, :], 0.0).then_inc(masks_zeroed, 1)
            made = zeroed = reduced = 0

            def cores_together():
                for semaphore, count in ((pads_zeroed, zeroed), (masks_made, made), (absmax_all, reduced)):
                    if count:
                        pool.wait_ge(semaphore, count)

            def zero(*paddings):
                nonlocal zeroed
                for padding in paddings:
                    cores_together()
                    nc.gpsimd.memset(padding, 0.0).then_inc(pads_zeroed, 1)
                    zeroed += 1

            def diagonal(m, pattern, base, fill):
                nonlocal made
                cores_together()
                nc.gpsimd.affine_select(out=m, in_=m, compare_op=ALU.not_equal, fill=fill, base=base,
                                        pattern=pattern, channel_multiplier=1).then_inc(masks_made, 1)
                made += 1

            def largest(n):
                nonlocal reduced
                cores_together()
                pool.wait_ge(absmax_ready, n + 1)
                nc.gpsimd.partition_all_reduce(wstat[:, n + 2:n + 3], wstat[:, n:n + 1], P,
                                               bass.bass_isa.ReduceOp.max).then_inc(absmax_all, 1)
                reduced += 1

            zero(wpad[:, :, 0:5:4, :])
            pool.wait_ge(masks_zeroed, 2)
            diagonal(ident[:, :], [[-1, C]], 0, 1.0)
            for other_half in (0, C, -C):
                diagonal(same_channel[:, :], [[-1, P]], other_half, 0.5 / GRP)
            assert made == MASKS
            largest(0)
            for n in range(2):
                zero(act[0:C, n, 0, :], act[C:P, n, KB - 1, :],
                     hi[0:C, n, 0, :])
                assert zeroed == (PADS_0, PADS_1)[n]
            largest(1)

        @block.scalar
        def _(sc):
            def split_hi(ph, i, r):
                k = r % 2
                sc.wait_ge(act_ready[ph], i + 1)
                if r >= 2:
                    sc.wait_ge(pair_done[ph][1], i - 1)
                nc.scalar.copy(hi[:, k, :], act[:, k]).then_inc(hi_ready[ph], 1)

            def normalise(ph, i, r, rows, func, scale, bias):
                k = r % 2
                if r >= 2:
                    sc.wait_ge(lo_ready[ph], i - 1)
                nc.scalar.activation(act[:, k, 1:J, :], rows(0, P, 1, J), func, bias=bias(0, P), scale=scale(0, P))
                nc.scalar.activation(act[C:P, k, 0, :], rows(C, P, 0, 1), func, bias=bias(C, P), scale=scale(C, P))
                nc.scalar.activation(act[0:C, k, J, :], rows(0, C, J, KB), func, bias=bias(0, C),
                                     scale=scale(0, C)).then_inc(act_ready[ph], 1)

            def halves(ph, i, func, rows, scale, bias):
                k = i % 2
                if i >= 2:
                    sc.wait_ge(pair_done[ph][1], i - 1)
                nc.scalar.activation(hi[C:P, k, 0], rows(C, P, 0, 1), func, bias=bias(C, P), scale=scale(C, P))
                nc.scalar.activation(hi[:, k, 1:HALF], rows(0, P, 1, HALF), func, bias=bias(0, P),
                                     scale=scale(0, P)).then_inc(half_hi[ph], 1)
                if i >= 2:
                    sc.wait_ge(lo_ready[ph], i - 1)
                nc.scalar.activation(act[:, k, HALF:J, :], rows(0, P, HALF, J), func, bias=bias(0, P), scale=scale(0, P))
                nc.scalar.activation(act[0:C, k, J, :], rows(0, C, J, KB), func, bias=bias(0, C),
                                     scale=scale(0, C)).then_inc(act_ready[ph], 1)
                sc.wait_ge(act_ready[ph], i + 1)
                nc.scalar.copy(hi[:, k, HALF:KB], act[:, k, HALF:KB]).then_inc(hi_ready[ph], 1)

            def x_args(r):
                m = r % 2

                def rows(a, b, k0, k1):
                    ap = xin[a:b, xin_rows(r % 4, k0, k1), :]
                    return ap.rearrange("p k w -> p (k w)") if k1 - k0 == 1 else ap
                return rows, lambda a, b: gn_s[a:b, m:m + 1], lambda a, b: gn_b[a:b, m:m + 1]

            def halves_x(i):
                sc.wait_ge(gn_coef_ready, i + 1 if i < 2 else i + 2)
                rows, scale, bias = x_args(i)
                halves(0, i, ACT.Identity, rows, scale, bias)

            def normalise_x(i, r):
                m = r % 2
                sc.wait_ge(gn_coef_ready, i + 2 - m)
                rows, scale, bias = x_args(r)
                normalise(0, i, r, rows, ACT.Identity, scale, bias)

            def halves_y1():
                sc.wait_ge(stage_stored[0][0], 16 * SPILL + 32)
                halves(1, 0, ACT.Relu, lambda a, b, k0, k1: slots_sb[a:b, k0:k1, :],
                       lambda a, b: A1[a:b, :], lambda a, b: B1[a:b, :])

            def normalise_y1(i, r):
                if r >= RES:
                    sc.wait_ge(y1_loaded[r % 4], i * 8 + (32 - 8 * (r % 4) - 8 * RES))
                else:
                    sc.wait_ge(stage_stored[0][r % 2], (i - r % 2) * 16 + (16 * SPILL + 32))
                base = slot_row(i if r < RES else i - RES, r % RES)
                normalise(1, i, r, lambda a, b, k0, k1: slots_sb[a:b, bass.ds(base + k0, k1 - k0), :],
                          ACT.Relu, lambda a, b: A1[a:b, :], lambda a, b: B1[a:b, :])

            def evacuate(ph, i, r, p):
                b = r % 2
                if p == 0 and r >= 2:
                    sc.wait_ge(stage_stored[ph][b], (i - b) * (16 if ph == 0 else 32))
                    sc.wait_ge(stage_read[ph], i - 1)
                if p == 0 and r < 2 and ph == 1:
                    sc.wait_ge(stage_stored[0][b], 16 * NIMG)
                sc.wait_ge(pair_done[ph][p], i + 1)
                rows = 2 * ROWS_PER_BANK
                nc.scalar.activation(
                    stage[:, b, p * rows:(p + 1) * rows, :].rearrange("q (n j) w -> q n (j w)", n=2),
                    conv_ps[:, 2 * p:2 * p + 2, 0:CH], ACT.Identity, bias=par[:, 3 * ph:3 * ph + 1],
                    scale=evac_scale[:, ph:ph + 1]).then_inc(pair_evac[ph][p], 1)

            def gn_sqrt(i, r):
                sc.wait_ge(gn_var_ready, i + 5)
                nc.scalar.activation(gn_sd[:, :], gn_var[:, :], ACT.Sqrt).then_inc(gn_sd_ready, 2)

            def gn_sqrt_of(m):
                sc.wait_ge(gn_var_ready, m + 1)
                nc.scalar.activation(gn_sd[:, m:m + 1], gn_var[:, m:m + 1], ACT.Sqrt, scale=-1.0).then_inc(gn_sd_ready, 1)

            def pass1(i, r):
                if r + 1 < NIMG:
                    split_hi(0, i + 1, r + 1)
                if r + 2 < NIMG:
                    normalise_x(i + 2, r + 2)
                evacuate(0, i, r, 0)
                if r % 2 == 1 and r + 4 < NIMG:
                    gn_sqrt(i, r)
                evacuate(0, i, r, 1)

            sc.wait_ge(pads_zeroed, PADS_W)
            nc.scalar.activation(warm[:, :], wpad[:, 0, 0, 0:1], ACT.Sqrt)
            sc.wait_ge(transposed, 1)
            nc.scalar.copy(wmat[0][:, :, :, :], wt_ps[0][:, :, :, :]).then_inc(wmat_ready, 1)
            gn_sqrt_of(0)
            sc.wait_ge(pads_zeroed, PADS_0)
            halves_x(0)
            gn_sqrt_of(1)
            sc.wait_ge(pads_zeroed, PADS_1)
            sc.wait_ge(params_loaded, 12 * 16)
            sc.wait_ge(evac_scale_ready, 1)
            evacuate(0, 0, 0, 0)
            halves_x(1)
            evacuate(0, 0, 0, 1)
            evacuate(0, 1, 1, 0)
            gn_sqrt(-1, -1)
            halves_x(2)
            evacuate(0, 1, 1, 1)
            normalise_x(3, 3)
            split_hi(0, 3, 3)
            evacuate(0, 2, 2, 0)
            gn_sqrt(1, 1)
            evacuate(0, 2, 2, 1)
            normalise_x(4, 4)
            evacuate(0, 3, 3, 0)
            split_hi(0, 4, 4)
            evacuate(0, 3, 3, 1)
            normalise_x(5, 5)
            gn_sqrt(3, 3)
            run_slots(sc, 4, NIMG - BODY, pass1)
            run_slots(sc, NIMG - BODY, NIMG, pass1)

            def bn_sqrt(ph):
                sc.wait_ge(bn_var_ready[ph], 1)
                nc.scalar.activation(bn_sd[:, ph:ph + 1], bn_w[:, ph, 3:4], ACT.Sqrt, scale=-1.0).then_inc(bn_sd_ready[ph], 1)

            bn_sqrt(0)
            sc.wait_ge(bn_coef_ready[0], 1)
            sc.wait_ge(evac_scale_ready, 2)

            def pass2(i, r):
                if r + 1 < NIMG and r >= 0:
                    split_hi(1, i + 1, r + 1)
                if r + 2 < NIMG:
                    normalise_y1(i + 2, r + 2)
                if r >= 0:
                    evacuate(1, i, r, 0)
                    evacuate(1, i, r, 1)

            halves_y1()
            run_slots(sc, -1, 2, pass2)
            run_slots(sc, 2, SPILL - 2, pass2)
            run_slots(sc, SPILL - 2, RES - 2, pass2)
            run_slots(sc, RES - 2, NIMG - 2, pass2)
            run_slots(sc, NIMG - 2, NIMG, pass2)
            bn_sqrt(1)
            sc.wait_ge(skip_coef, 3)

            def pass3(q, r):
                if r >= RES:
                    sc.wait_ge(y2_loaded[r % 4], q * 8 + (32 - 8 * (r % 4) - 8 * RES))
                if r < SPILL:
                    sc.wait_ge(stage_stored[1][r % 2], (q - r % 2) * 32 + (32 * RES + 64))
                base = slot_row(q if r < RES else q - RES, r % RES)
                img = image_of(q, r)
                slot = slots_sb[:, bass.ds(base, J), :]
                nc.scalar.activation(slot, slot, ACT.Identity,
                                     bias=skip_b[:, bass.ds(img, 1)], scale=A2).then_inc(u_ready, 1)

            run_slots(sc, 0, SPILL, pass3)
            run_slots(sc, SPILL, RES, pass3)
            run_slots(sc, RES, NIMG, pass3)

        @block.vector
        def _(dve):
            steps = 0

            def setup_step(ins):
                nonlocal steps
                steps += 1
                ins.then_inc(wprep, 1)
                dve.wait_ge(wprep, steps)

            def weight_absmax(n):
                dve.wait_ge(weights_loaded[n], 32)
                nc.vector.tensor_reduce(wstat[:, n:n + 1], wraw[:, :], AX.X, ALU.max,
                                        apply_absolute_value=True).then_inc(absmax_ready, 1)

            def quantise(n):
                dve.wait_ge(absmax_all, n + 1)
                setup_step(nc.vector.tensor_scalar(qscale[:, n:n + 1], wstat[:, n + 2:n + 3], 1.0 / QMAX, None, ALU.mult))
                setup_step(nc.vector.reciprocal(wstat[:, n + 4:n + 5], qscale[:, n:n + 1]))
                setup_step(nc.vector.tensor_scalar(wraw[0:C, :], wraw[0:C, :], wstat[0:C, n + 4:n + 5], ROUND,
                                                   ALU.mult, ALU.add))
                dve.wait_ge(pads_zeroed, PADS_W)
                nc.vector.tensor_scalar(
                    wpad[:, :, 1:4, :].rearrange("o kx ky i -> o i ky kx"),
                    wraw[0:C, :].rearrange("o (i ky kx) -> o i ky kx", ky=3, kx=3), ROUND, None,
                    ALU.subtract).then_inc(quantised, 1)
                nc.vector.tensor_scalar(evac_scale[:, n:n + 1], qscale[:, n:n + 1],
                                        1.0 / (GN_SCALE, BN_SCALE)[n], None, ALU.mult).then_inc(evac_scale_ready, 1)

            def power_of_two():
                dve.wait_ge(params_loaded, 12 * 16)
                setup_step(nc.vector.tensor_reduce(pabs[:, 0:1], par[:, 1:3], AX.X, ALU.add, apply_absolute_value=True))
                setup_step(nc.vector.tensor_scalar(pabs[:, 1:2].bitcast(U32), pabs[:, 0:1].bitcast(U32), 0x7F800000, None,
                                                   ALU.bitwise_and))
                setup_step(nc.vector.tensor_scalar(pow2[:, 0:1], pabs[:, 1:2], 2.0 ** -60, None, ALU.max))
                setup_step(nc.vector.reciprocal(pabs[:, 0:1], pow2[:, 0:1]))
                setup_step(nc.vector.tensor_scalar(pow2[:, 1:2], pabs[:, 0:1], BN_SCALE, None, ALU.mult))
                setup_step(nc.vector.tensor_scalar(bn_affine[:, 0, 0:1], par[:, 1:2], 0.5, pow2[:, 1:2], ALU.mult, ALU.mult))
                setup_step(nc.vector.tensor_scalar(bn_affine[:, 0, 1:2], par[:, 2:3], pow2[:, 1:2], None, ALU.mult))
                setup_step(nc.vector.tensor_scalar(bn_affine[:, 1, 0:1], par[:, 4:5], 0.5, None, ALU.mult))
                setup_step(nc.vector.tensor_copy(bn_affine[:, 1, 1:2], par[:, 5:6]))

            def averages():
                dve.wait_ge(masks_made, MASKS)
                pairs = same_channel[:, :].rearrange("p (g e) -> p g e", e=GRP)
                for e in range(GRP):
                    ins = nc.vector.tensor_tensor(gn_avg[:, :].rearrange("p (g e) -> p g e", e=GRP)[:, :, e],
                                                  pairs[:, :, 0], pairs[:, :, 1], ALU.add)
                ins.then_inc(averages_made, 1)

            def bn_average():
                nc.vector.tensor_scalar(bn_avg[:, :], same_channel[:, :], GRP * BODY / NIMG, None,
                                        ALU.mult).then_inc(averages_made, 1)

            def conv2_matrix():
                dve.wait_ge(transposed, 2)
                nc.vector.tensor_scalar(wmat[1][:, :, :, :], wt_ps[1][:, :, :, :], pow2[:, 0:1], None,
                                        ALU.mult).then_inc(wmat_ready, 1)

            def gn_stats(i, r):
                b, m = r % 4, r % 2
                if r == 0:
                    dve.wait_ge(x0_first_rows, 32)
                else:
                    dve.wait_ge(x_loaded[b], i * 8 + (32 - 8 * b))
                if m == 0 and r >= 2:
                    dve.wait_ge(gn_moments, i)
                for t in range(3):
                    if r == 0 and t == 2:
                        dve.wait_ge(x_loaded[b], 32)
                    nc.vector.bn_stats(gn_tup[:, m, t, :], xin[:, xin_rows(b, 1 + t * third, 1 + (t + 1) * third), :].rearrange("p k w -> p (k w)"))
                nc.vector.bn_stats(gn_tup[C:P, m, 3, :], xin[C:P, b * J, :])
                nc.vector.bn_stats(gn_tup[0:C, m, 3, :], xin[0:C, b * J + J, :]).then_inc(gn_tuples, 1)


            def gn_chain_a(i, r):
                dve.wait_ge(gn_tuples, i + 1)
                if r >= 3:
                    dve.wait_ge(gn_combined, i - 1)
                nc.vector.memset(gn_sq[:, :], 0.0)
                for m in range(2):
                    ins = nc.vector.bn_aggr(gn_mv[:, m, :], gn_tup[:, m].rearrange("p a b -> p (a b)"))
                ins.then_inc(gn_step_a, 1)
                dve.wait_ge(gn_step_a, i - 2)
                nc.vector.tensor_tensor(gn_sq[:, :], gn_mv[:, :, 0], gn_mv[:, :, 0], ALU.mult).then_inc(gn_step_a, 1)
                dve.wait_ge(gn_step_a, i - 1)
                nc.vector.tensor_tensor(gn_mv[:, :, 1], gn_mv[:, :, 1], gn_sq[:, :], ALU.add).then_inc(gn_moments, 2)

            B1_STEPS, B2_STEPS = 3, 7

            def chain(semaphore, base):
                n = 0

                def step(ins):
                    nonlocal n
                    n += 1
                    ins.then_inc(semaphore, 1)
                    dve.wait_ge(semaphore, base + n)
                return step

            def gn_chain_b1(i, r):
                step = chain(gn_step_b, (i - 3) * 5)
                dve.wait_ge(gn_combined, i + 1)
                step(nc.vector.tensor_copy(gn_g[:, :, :].rearrange("p a b -> p (a b)"), stat_ps[:, 0:4]))
                step(nc.vector.tensor_tensor(gn_tmp[:, 0, :], gn_g[:, :, 0], gn_g[:, :, 0], ALU.mult))
                step(nc.vector.tensor_tensor(gn_tmp[:, 1, :], gn_g[:, :, 1], gn_tmp[:, 0, :], ALU.subtract))
                nc.vector.tensor_scalar(gn_var[:, :], gn_tmp[:, 1, :], 0.0, GN_EPS, ALU.max, ALU.add).then_inc(gn_var_ready, 2)

            def gn_chain_b2(i, r):
                step = chain(gn_step_b, (i - 3) * 5 + B1_STEPS)
                dve.wait_ge(gn_sd_ready, i + 1)
                step(nc.vector.reciprocal(gn_tmp[:, 2, :], gn_sd[:, :]))
                step(nc.vector.tensor_tensor(gn_tmp[:, 0, :], gn_tmp[:, 2, :], gn_tmp[:, 2, :], ALU.mult))
                step(nc.vector.tensor_tensor(gn_tmp[:, 1, :], gn_tmp[:, 0, :], gn_var[:, :], ALU.mult))
                step(nc.vector.tensor_scalar(gn_tmp[:, 3, :], gn_tmp[:, 1, :], -0.5 * GN_SCALE, 1.5 * GN_SCALE, ALU.mult, ALU.add))
                if r >= 3:
                    dve.wait_ge(act_ready[0], i - 1)
                step(nc.vector.tensor_tensor(gn_s[:, :], gn_tmp[:, 3, :], gn_tmp[:, 2, :], ALU.mult))
                nc.vector.scalar_tensor_tensor(out=gn_b[:, :], in0=gn_g[:, :, 0], scalar=-1.0, in1=gn_s[:, :],
                                               op0=ALU.mult, op1=ALU.mult).then_inc(gn_coef_ready, 2)
                step(nc.vector.tensor_copy(gn_s_all[:, bass.ds(i - 1, 2)], gn_s[:, :]))
                dve.wait_ge(gn_coef_ready, i + 1)
                step(nc.vector.tensor_copy(gn_b_all[:, bass.ds(i - 1, 2)], gn_b[:, :]))

            def gn_first_a(m):
                mean, second = gn_mv[:, m, 0:1], gn_mv[:, m, 1:2]
                dve.wait_ge(gn_tuples, m + 1)
                nc.vector.memset(gn_sq[:, m:m + 1], 0.0)
                setup_step(nc.vector.bn_aggr(gn_mv[:, m, :], gn_tup[:, m].rearrange("p a b -> p (a b)")))
                nc.vector.scalar_tensor_tensor(out=second, in0=mean, scalar=mean, in1=second,
                                               op0=ALU.mult, op1=ALU.add).then_inc(gn_moments, 1)

            def gn_first_b1(m):
                mean = gn_g[:, m, 0:1]
                dve.wait_ge(gn_combined, m + 1)
                setup_step(nc.vector.tensor_copy(gn_g[:, m, :], stat_ps[:, 2 * m:2 * m + 2]))
                setup_step(nc.vector.scalar_tensor_tensor(out=gn_tmp[:, 0, m:m + 1], in0=mean, scalar=mean,
                                                          in1=gn_g[:, m, 1:2], op0=ALU.mult, op1=ALU.subtract))
                nc.vector.tensor_scalar(gn_var[:, m:m + 1], gn_tmp[:, 0, m:m + 1], 0.0, GN_EPS, ALU.min,
                                        ALU.subtract).then_inc(gn_var_ready, 1)

            def gn_first_b2(m):
                root, correction, scale = gn_tmp[:, 2, m:m + 1], gn_tmp[:, 1, m:m + 1], gn_s[:, m:m + 1]
                dve.wait_ge(gn_sd_ready, m + 1)
                setup_step(nc.vector.reciprocal(root, gn_sd[:, m:m + 1]))
                setup_step(nc.vector.scalar_tensor_tensor(out=correction, in0=root, scalar=root, in1=gn_var[:, m:m + 1],
                                                          op0=ALU.mult, op1=ALU.mult))
                setup_step(nc.vector.tensor_scalar(gn_tmp[:, 3, m:m + 1], correction, 0.5 * GN_SCALE, 1.5 * GN_SCALE,
                                                   ALU.mult, ALU.add))
                setup_step(nc.vector.tensor_tensor(scale, gn_tmp[:, 3, m:m + 1], root, ALU.mult))
                nc.vector.scalar_tensor_tensor(out=gn_b[:, m:m + 1], in0=gn_g[:, m, 0:1], scalar=-1.0, in1=scale,
                                               op0=ALU.mult, op1=ALU.mult).then_inc(gn_coef_ready, 1)
                dve.wait_ge(gn_coef_ready, m + 1)
                nc.vector.tensor_copy(gn_s_all[:, m:m + 1], scale)
                nc.vector.tensor_copy(gn_b_all[:, m:m + 1], gn_b[:, m:m + 1])

            def half_lo_x(i):
                k, m = i % 2, i % 2
                for a, b, k0, k1 in ((C, P, 0, 1), (0, P, 1, HALF)):
                    ins = nc.vector.tensor_scalar(act[a:b, k, k0:k1, :], xin[a:b, xin_rows(i % 4, k0, k1), :], gn_s[a:b, m:m + 1],
                                                  gn_b[a:b, m:m + 1], ALU.mult, ALU.add)
                ins.then_inc(half_act[0], 1)
                dve.wait_ge(half_act[0], i + 1)
                dve.wait_ge(half_hi[0], i + 1)
                nc.vector.tensor_tensor(lo[:, k, 0:HALF], act[:, k, 0:HALF], hi[:, k, 0:HALF],
                                        ALU.subtract).then_inc(half_lo[0], 1)

            def half_lo_y1():
                for a, b, k0, k1 in ((C, P, 0, 1), (0, P, 1, HALF)):
                    ins = nc.vector.tensor_scalar(act[a:b, 0, k0:k1, :], slots_sb[a:b, k0:k1, :], A1[a:b, :], B1[a:b, :],
                                                  ALU.mult, ALU.add)
                ins.then_inc(half_act[1], 1)
                dve.wait_ge(half_act[1], 1)
                dve.wait_ge(half_hi[1], 1)
                nc.vector.scalar_tensor_tensor(out=lo[:, 0, 0:HALF], in0=act[:, 0, 0:HALF], scalar=0.0,
                                               in1=hi[:, 0, 0:HALF], op0=ALU.max,
                                               op1=ALU.subtract).then_inc(half_lo[1], 1)

            def rest_lo(ph, i):
                dve.wait_ge(hi_ready[ph], i + 1)
                nc.vector.tensor_tensor(lo[:, i % 2, HALF:KB], act[:, i % 2, HALF:KB], hi[:, i % 2, HALF:KB],
                                        ALU.subtract).then_inc(lo_ready[ph], 1)

            def split_lo(ph, i, r):
                k = r % 2
                dve.wait_ge(hi_ready[ph], i + 1)
                nc.vector.tensor_tensor(lo[:, k, :], act[:, k], hi[:, k, :], ALU.subtract).then_inc(lo_ready[ph], 1)

            def bn_stats(ph, i, r, p):
                dve.wait_ge(pair_evac[ph][p], i + 1)
                if r % BODY == 0 and p == 0 and r >= BODY:
                    dve.wait_ge(bn_sums[ph], i)
                rows = ROWS_PER_BANK
                for c in range(2 * p, 2 * p + 2):
                    ins = nc.vector.bn_stats(bn_tup[:, (r % BODY) * NCH + c, :],
                                             stage[:, r % 2, c * rows:(c + 1) * rows, :].rearrange("q j w -> q (j w)"))
                if p == NPAIR - 1:
                    ins.then_inc(stage_read[ph], 1)

            def bn_accumulate(ph, i, r):
                base = i - (BODY - 1)
                mean, second = bn_mv[:, 0:1], bn_mv[:, 1:2]
                dve.wait_ge(stage_read[ph], i + 1)
                nc.vector.memset(bn_sq[:, :], 0.0)
                nc.vector.bn_aggr(bn_mv[:, :], bn_tup[:, :, :].rearrange("p a b -> p (a b)")).then_inc(bn_step[ph], BODY // 2)
                dve.wait_ge(bn_step[ph], base + BODY // 2)
                nc.vector.scalar_tensor_tensor(out=second, in0=mean, scalar=mean, in1=second, op0=ALU.mult,
                                               op1=ALU.add).then_inc(bn_step[ph], BODY // 2)
                dve.wait_ge(bn_step[ph], base + BODY)
                nc.vector.tensor_tensor(bn_acc[ph][:, :], bn_acc[ph][:, :], bn_mv[:, :], ALU.add).then_inc(bn_sums[ph], BODY)

            def bn_coefficients(ph):
                step = chain(bn_chain[ph], 0)
                v = lambda c: bn_w[:, ph, c:c + 1]
                mean, neg_mean, neg_var, root = v(0), v(4), v(3), v(5)
                half_gamma, beta = bn_affine[:, ph, 0:1], bn_affine[:, ph, 1:2]
                dve.wait_ge(bn_combined[ph], 1)
                step(nc.vector.tensor_copy(bn_w[:, ph, 0:2], stat_ps[:, 0:2]))
                step(nc.vector.scalar_tensor_tensor(out=v(2), in0=mean, scalar=mean, in1=v(1), op0=ALU.mult, op1=ALU.subtract))
                nc.vector.tensor_scalar(neg_var, v(2), 0.0, BN_EPS, ALU.min, ALU.subtract).then_inc(bn_var_ready[ph], 1)
                step(nc.vector.tensor_scalar(neg_mean, mean, -1.0, None, ALU.mult))
                dve.wait_ge(bn_sd_ready[ph], 1)
                step(nc.vector.reciprocal(root, bn_sd[:, ph:ph + 1]))
                nc.vector.tensor_tensor(v(7), root, half_gamma, ALU.mult)
                step(nc.vector.scalar_tensor_tensor(out=v(6), in0=root, scalar=root, in1=neg_var, op0=ALU.mult, op1=ALU.mult))
                step(nc.vector.scalar_tensor_tensor(out=v(8), in0=v(6), scalar=3.0, in1=v(7), op0=ALU.add, op1=ALU.mult))
                shift = nc.vector.scalar_tensor_tensor(out=v(9), in0=v(8), scalar=neg_mean, in1=beta, op0=ALU.mult, op1=ALU.add)
                if ph == 0:
                    shift.then_inc(bn_coef_ready[0], 1)
                else:
                    step(shift)
                    nc.vector.tensor_scalar(skip_b[:, :], gn_b_all[:, :], v(9), None, ALU.add).then_inc(skip_coef, 1)

            def skip_coefficients():
                nc.vector.tensor_scalar(skip_s[:, :], gn_s_all[:, :], 1.0 / GN_SCALE, None, ALU.mult).then_inc(skip_coef, 1)
                nc.vector.tensor_scalar(gn_b_all[:, :], gn_b_all[:, :], 1.0 / GN_SCALE, None, ALU.mult).then_inc(skip_coef, 1)
                dve.wait_ge(skip_coef, 2)

            def lo_and_last_bn(ph, i, r):
                if r >= 1:
                    bn_stats(ph, i - 1, r - 1, 1)
                if 0 <= r + 1 < NIMG:
                    split_lo(ph, i + 1, r + 1)
                if r >= 1 and r % BODY == 0:
                    bn_accumulate(ph, i - 1, r - 1)

            def pass1(i, r):
                pair_complete = r % 2 == 1 and r + 4 < NIMG
                if r + 4 < NIMG:
                    gn_stats(i + 4, r + 4)
                if pair_complete:
                    gn_chain_a(i + 4, r + 4)
                lo_and_last_bn(0, i, r)
                if pair_complete:
                    gn_chain_b1(i + 4, r + 4)
                if r < NIMG:
                    bn_stats(0, i, r, 0)
                if pair_complete:
                    gn_chain_b2(i + 4, r + 4)

            weight_absmax(0)
            for n in range(2):
                setup_step(nc.vector.memset(bn_acc[n][:, :], 0.0))
            quantise(0)
            averages()
            gn_stats(0, 0)
            gn_first_a(0)
            gn_first_b1(0)
            gn_first_b2(0)
            dve.wait_ge(pads_zeroed, PADS_1)
            half_lo_x(0)
            gn_stats(1, 1)
            gn_first_a(1)
            rest_lo(0, 0)
            gn_first_b1(1)
            gn_first_b2(1)
            half_lo_x(1)
            gn_stats(2, 2)
            rest_lo(0, 1)
            gn_stats(3, 3)
            gn_chain_a(3, 3)
            bn_stats(0, 0, 0, 0)
            gn_chain_b1(3, 3)
            gn_chain_b2(3, 3)
            half_lo_x(2)
            rest_lo(0, 2)
            bn_stats(0, 0, 0, 1)
            gn_stats(4, 4)
            split_lo(0, 3, 3)
            gn_stats(5, 5)
            gn_chain_a(5, 5)
            bn_stats(0, 1, 1, 0)
            gn_chain_b1(5, 5)
            gn_chain_b2(5, 5)
            bn_stats(0, 1, 1, 1)
            gn_stats(6, 6)
            bn_stats(0, 2, 2, 0)
            run_slots(dve, 3, BODY, pass1)
            run_slots(dve, BODY, NIMG - BODY, pass1)
            bn_average()
            weight_absmax(1)
            power_of_two()
            run_slots(dve, NIMG - BODY, NIMG - BODY + 1, pass1)
            quantise(1)
            run_slots(dve, NIMG - BODY + 1, NIMG - 1, pass1)
            conv2_matrix()
            run_slots(dve, NIMG - 1, NIMG + 1, pass1)
            bn_coefficients(0)

            def pass2(i, r):
                lo_and_last_bn(1, i, r)
                if 0 <= r < NIMG:
                    bn_stats(1, i, r, 0)

            dve.wait_ge(bn_coef_ready[0], 1)
            half_lo_y1()
            rest_lo(1, 0)
            run_slots(dve, 0, BODY, pass2)
            run_slots(dve, BODY, NIMG - BODY, pass2)
            skip_coefficients()
            run_slots(dve, NIMG - BODY, NIMG + 1, pass2)
            bn_coefficients(1)

            def pass3(q, r):
                img = image_of(q, r)
                xs = x3_buffer(r)
                if r < OWN:
                    dve.wait_ge(x3_own_loaded[r], 32)
                else:
                    dve.wait_ge(x3_loaded[r % 4], (q - first_use(r % 4)) * 8 + 32)
                u = slots_sb[:, bass.ds(slot_row(q if r < RES else q - RES, r % RES), J), :].rearrange("p j w -> p (j w)")
                dve.wait_ge(u_ready, q + 1)
                nc.vector.scalar_tensor_tensor(out=u, in0=xs, scalar=skip_s[:, bass.ds(img, 1)], in1=u,
                                               op0=ALU.mult, op1=ALU.add).then_inc(sum_ready, 1)
                dve.wait_ge(sum_ready, q + 1)
                nc.vector.scalar_tensor_tensor(out=u, in0=u, scalar=0.0, in1=xs,
                                               op0=ALU.max, op1=ALU.add).then_inc(out_ready, 1)

            for q in range(RES - BODY):
                pass3(q, q)
            run_slots(dve, RES - BODY, RES, pass3)
            run_slots(dve, RES, NIMG, pass3)

        @block.tensor
        def _(pe):
            pe.wait_ge(masks_made, 1)

            def weight_transposes(n):
                pe.wait_ge(quantised, n + 1)
                for kx in range(3):
                    for pair, o, ky in ((0, 0, 1), (0, 1, 0), (1, 0, 3), (1, 1, 2)):
                        mm = nc.tensor.transpose(wt_ps[n][:, kx, pair, o * C:(o + 1) * C],
                                                 wpad[:, kx, ky:ky + 2, :].rearrange("o a i -> o (a i)"), ident[:, :])
                mm.then_inc(transposed, 1)

            weight_transposes(0)

            def gn_combine(i, r):
                pe.wait_ge(gn_moments, i + 1)
                if r >= 3:
                    pe.wait_ge(gn_var_ready, i - 1)
                nc.tensor.matmul(stat_ps[:, 0:4], gn_avg[:, :], gn_mv[:, :, :].rearrange("p a b -> p (a b)"),
                                 start=True, stop=True).then_inc(gn_combined, 2)

            TAPS = ((1, 0), (0, 0), (0, 1), (2, 0), (2, 1), (1, 1))
            conv_rows = conv_ps[:, :, 0:CH].rearrange("p c (r w) -> p c r w", w=W)

            def conv(ph, i, r, between=None, at=(0, 5)):
                k = r % 2
                halves = r < DIRECT[ph]
                for p in range(NPAIR):
                    if halves and p == 0:
                        pe.wait_ge(half_lo[ph], i + 1)
                    elif halves or p == 0:
                        pe.wait_ge(hi_ready[ph], i + 1)
                        pe.wait_ge(lo_ready[ph], i + 1)
                    if r >= 1:
                        pe.wait_ge(pair_evac[ph][p], i)
                    for n, (kx, pair) in enumerate(TAPS):
                        w0, w1 = max(0, 1 - kx), min(W, W + 1 - kx)
                        for part in (hi, lo):
                            for c in range(2 * p, 2 * p + 2):
                                k0 = c * ROWS_PER_BANK + pair
                                mm = nc.tensor.matmul(conv_rows[:, c, :, w0:w1], wmat[ph][:, kx, pair, :],
                                                      part[:, k, k0:k0 + ROWS_PER_BANK, w0 + kx - 1:w1 + kx - 1],
                                                      start=n == 0 and part is hi, stop=n == 5 and part is lo)
                        if n == 5:
                            mm.then_inc(pair_done[ph][p], 1)
                        if between and (p, n) == at:
                            between()

            def gn_combine_of(m):
                pe.wait_ge(gn_moments, m + 1)
                nc.tensor.matmul(stat_ps[:, 2 * m:2 * m + 2], gn_avg[:, :], gn_mv[:, m, :],
                                 start=True, stop=True).then_inc(gn_combined, 1)

            def pass1(i, r):
                if r % 2 == 1 and r + 4 < NIMG:
                    conv(0, i, r, lambda: gn_combine(i + 4, r + 4))
                else:
                    conv(0, i, r)

            def keep_warm(n, count):
                for _ in range(count):
                    nc.tensor.matmul(conv_ps[:, 0, 0:CH], wmat[n][:, 0, 0, :],
                                     wmat[n][:, :, :, :].rearrange("p a b m -> p (a b m)")[:, 0:CH], start=True, stop=True)

            pe.wait_ge(averages_made, 1)
            pe.wait_ge(wmat_ready, 1)
            keep_warm(0, WARM0)
            gn_combine_of(0)
            keep_warm(0, WARM1)
            conv(0, 0, 0, lambda: gn_combine_of(1), at=(0, 3))
            conv(0, 1, 1, lambda: gn_combine(3, 3), at=(1, 1))
            conv(0, 2, 2)
            conv(0, 3, 3, lambda: gn_combine(5, 5), at=(0, 1))
            gn_combine(7, 7)
            run_slots(pe, BODY, NIMG - BODY, pass1)
            run_slots(pe, NIMG - BODY, NIMG - 2, pass1)
            weight_transposes(1)
            run_slots(pe, NIMG - 2, NIMG, pass1)

            pe.wait_ge(pair_evac[0][1], NIMG)
            pe.wait_ge(wmat_ready, 2)
            keep_warm(1, WARM2)

            def bn_combine(ph):
                pe.wait_ge(averages_made, 2)
                pe.wait_ge(bn_sums[ph], NIMG)
                nc.tensor.matmul(stat_ps[:, 0:2], bn_avg[:, :], bn_acc[ph][:, :], start=True, stop=True).then_inc(bn_combined[ph], 1)

            bn_combine(0)
            keep_warm(1, WARM3)
            run_slots(pe, 0, BODY, lambda i, r: conv(1, i, r))
            run_slots(pe, BODY, NIMG, lambda i, r: conv(1, i, r))
            bn_combine(1)


_INS = ['x', 'L0_conv_w1', 'L0_conv_b1', 'L0_conv_gamma1', 'L0_conv_beta1',
        'L0_conv_w2', 'L0_conv_b2', 'L0_conv_gamma2', 'L0_conv_beta2']


def kernel(**inputs):
    import numpy as _np
    import concourse.bacc as _bacc
    from concourse import mybir as _mybir
    from concourse.bass_utils import run_bass_kernel_spmd as _run

    nc = _bacc.Bacc("TRN2", target_bir_lowering=False, num_devices=1)
    arrays, args = {}, []
    for name in _INS:
        a = _np.ascontiguousarray(inputs[name])
        arrays[f"in_{name}_dram"] = a
        args.append(nc.dram_tensor(f"in_{name}_dram", a.shape, _mybir.dt.from_np(a.dtype), kind="ExternalInput").ap())
    shape = inputs["x"].shape
    args.append(nc.dram_tensor("out_0_dram", shape, _mybir.dt.float32, kind="ExternalOutput").ap())
    conv_block_kernel(nc, *args)
    r = _run(nc, [arrays], core_ids=[0])
    return r.results[0]["out_0_dram"]
```

```python
from contextlib import ExitStack

import concourse.bass as bass
from concourse import mybir

F32 = mybir.dt.float32
F16 = mybir.dt.float16
BF16 = mybir.dt.bfloat16
U32 = mybir.dt.uint32
ALU = mybir.AluOpType
ACT = mybir.ActivationFunctionType
AX = mybir.AxisListType

P = 128
BODY = 4
GN_EPS = 1e-5
BN_EPS = 1e-5
QMAX = 127.0
ROUND = 12582912.0
GN_SCALE = 512.0
BN_SCALE = 64.0


def conv_block_kernel(nc, x, w1, b1, g1, be1, w2, b2, g2, be2, out):
    NIMG, C, H, W = x.shape
    assert C == 64 and H % 2 == 0
    J = H // 2
    KB = J + 1
    PIX = J * W
    ROWS_PER_BANK = 7
    NCH = J // ROWS_PER_BANK
    CH = ROWS_PER_BANK * W
    NPAIR = NCH // 2
    HALF = 2 * ROWS_PER_BANK + 1
    DIRECT = (5, 1)
    assert NPAIR == 2 and J % (2 * ROWS_PER_BANK) == 0 and NIMG % BODY == 0 and CH <= 512
    RES = 20
    SPILL = NIMG - RES
    assert RES % BODY == 0 and SPILL % BODY == 0 and SPILL <= RES - BODY
    ALONE = 4
    GRP = 2

    with ExitStack() as ctx:
        def sb(name, shape, dt):
            return ctx.enter_context(nc.sbuf_tensor(name, shape, dt))

        def psum(name, shape, dt):
            return ctx.enter_context(nc.psum_tensor(name, shape, dt))

        def sem(name):
            return ctx.enter_context(nc.semaphore(name))

        y1_spill = nc.dram_tensor("y1_spill", [SPILL, P, PIX], F32, kind="Internal").ap()
        y2_spill = nc.dram_tensor("y2_spill", [SPILL, C, H, W], F32, kind="Internal").ap()

        slots_sb = sb("slots_sb", [P, RES * J + 2, W], F32)
        xin = sb("xin", [P, 4 * J + 1, W], F32)
        act = sb("act", [P, 2, KB, W], F32)
        spare = sb("spare", [P, PIX], F32)
        spare2 = sb("spare2", [P, PIX], F32)
        split = sb("split", [P, 2, 2, KB, W], F16)
        hi, lo = split[:, :, 0], split[:, :, 1]
        stage = sb("stage", [P, 2, J, W], F32)
        first_only = sb("first_only", [P, PIX], F32)
        cuts = [0, C * 9, C * 9 + 15 * C // 2, C * 9 + 15 * C // 2 + 3 * P, C * 9 + 15 * C // 2 + 4 * P]
        assert cuts[-1] <= PIX
        part = lambda n: first_only[:, cuts[n]:cuts[n + 1]]
        wraw = part(0)
        wpad = part(1).bitcast(BF16)[0:C].rearrange("o (x y i) -> o x y i", x=3, y=5)
        wmat = [part(2).bitcast(BF16).rearrange("p (x r m) -> p x r m", x=3, r=2), sb("wmat2", [P, 3, 2, P], BF16)]
        same_channel = part(3)
        gn_avg = spare2[:, 0:P]
        ident = spare2[0:C, P:P + C // 2].bitcast(BF16)
        bn_avg = sb("bn_avg", [P, P], F32)
        par = sb("par", [P, 6], F32)
        wstat = sb("wstat", [P, 8], F32)
        qscale = sb("qscale", [P, 2], F32)
        evac_scale = sb("evac_scale", [P, 2], F32)
        pow2 = sb("pow2", [P, 2], F32)
        pabs = sb("pabs", [P, 2], F32)
        warm = sb("warm", [C, 1], F32)
        gn_tup = sb("gn_tup", [P, 2, 4, 6], F32)
        gn_mv = sb("gn_mv", [P, 2, 2], F32)
        gn_sq = sb("gn_sq", [P, 2], F32)
        gn_g = sb("gn_g", [P, 2, 2], F32)
        gn_var = sb("gn_var", [P, 2], F32)
        gn_sd = sb("gn_sd", [P, 2], F32)
        gn_tmp = sb("gn_tmp", [P, 4, 2], F32)
        gn_s_all = sb("gn_s_all", [P, NIMG], F32)
        gn_b_all = sb("gn_b_all", [P, NIMG], F32)
        skip_s = sb("skip_s", [P, NIMG], F32)
        skip_b = sb("skip_b", [P, NIMG], F32)
        bn_tup = sb("bn_tup", [P, BODY * NCH, 6], F32)
        bn_mv = sb("bn_mv", [P, 2], F32)
        bn_sq = sb("bn_sq", [P, 1], F32)
        bn_acc = [sb(f"bn_acc{n}", [P, 2], F32) for n in (1, 2)]
        bn_w = sb("bn_w", [P, 2, 10], F32)
        bn_affine = sb("bn_affine", [P, 2, 2], F32)
        bn_sd = sb("bn_sd", [P, 2], F32)

        conv_ps = psum("conv_ps", [P, 4, 512], F32)
        stat_ps = psum("stat_ps", [P, 512], F32)
        wt_ps = [psum(f"wt_ps{n}", [P, 3, 2, P], BF16) for n in (1, 2)]

        params_loaded = sem("params_loaded")
        weights_loaded = [sem(f"weights_loaded{n}") for n in (1, 2)]
        masks_zeroed = sem("masks_zeroed")
        masks_made = sem("masks_made")
        pads_zeroed = sem("pads_zeroed")
        wprep = sem("wprep")
        absmax_ready = sem("absmax_ready")
        absmax_all = sem("absmax_all")
        quantised = sem("quantised")
        transposed = sem("transposed")
        wmat_ready = sem("wmat_ready")
        evac_scale_ready = sem("evac_scale_ready")
        averages_made = sem("averages_made")
        x0_first_rows = sem("x0_first_rows")
        x_loaded = [sem(f"x_loaded{b}") for b in range(4)]
        gn_tuples = sem("gn_tuples")
        gn_step_a = sem("gn_step_a")
        gn_scale_ready = sem("gn_scale_ready")
        gn_moments = sem("gn_moments")
        gn_combined = sem("gn_combined")
        gn_step_b = sem("gn_step_b")
        gn_var_ready = sem("gn_var_ready")
        gn_sd_ready = sem("gn_sd_ready")
        gn_coef_ready = sem("gn_coef_ready")
        half_act = [sem(f"half_act{n}") for n in (1, 2)]
        half_hi = [sem(f"half_hi{n}") for n in (1, 2)]
        half_lo = [sem(f"half_lo{n}") for n in (1, 2)]
        act_ready = [sem(f"act_ready{n}") for n in (1, 2)]
        hi_ready = [sem(f"hi_ready{n}") for n in (1, 2)]
        lo_ready = [sem(f"lo_ready{n}") for n in (1, 2)]
        pair_done = [[sem(f"pair_done{n}_{p}") for p in range(2)] for n in (1, 2)]
        pair_evac = [[sem(f"pair_evac{n}_{p}") for p in range(2)] for n in (1, 2)]
        chunk_done = [sem(f"chunk_done{n}") for n in (1, 2)]
        chunk_evac = [sem(f"chunk_evac{n}") for n in (1, 2)]
        stage_read = [sem(f"stage_read{n}") for n in (1, 2)]
        stage_stored = [[sem(f"stage_stored{n}_{b}") for b in range(2)] for n in (1, 2)]
        bn_step = [sem(f"bn_step{n}") for n in (1, 2)]
        bn_sums = [sem(f"bn_sums{n}") for n in (1, 2)]
        bn_combined = [sem(f"bn_combined{n}") for n in (1, 2)]
        bn_chain = [sem(f"bn_chain{n}") for n in (1, 2)]
        bn_var_ready = [sem(f"bn_var_ready{n}") for n in (1, 2)]
        bn_sd_ready = [sem(f"bn_sd_ready{n}") for n in (1, 2)]
        bn_coef_ready = [sem(f"bn_coef_ready{n}") for n in (1, 2)]
        y1_loaded = [sem(f"y1_loaded{b}") for b in range(4)]
        skip_coef = sem("skip_coef")
        x3_own_loaded = [sem(f"x3_own_loaded{q}") for q in range(13)]
        x3_loaded = [sem(f"x3_loaded{b}") for b in range(4)]
        y2_loaded = [sem(f"y2_loaded{b}") for b in range(4)]
        u_ready = sem("u_ready")
        sum_ready = sem("sum_ready")
        out_ready = sem("out_ready")
        half_u = sem("half_u")
        half_sum = sem("half_sum")
        half_out = sem("half_out")
        half_stored = sem("half_stored")
        out_stored = [sem(f"out_stored{b}") for b in range(4)]

        A1, B1, A2 = bn_w[:, 0, 8:9], bn_w[:, 0, 9:10], bn_w[:, 1, 8:9]

        def odd_even(ap):
            return ap.rearrange("c (j h) w -> h c j w", h=2)

        def run_slots(eng, start, stop, body):
            n = (stop - start) // BODY
            if n >= 2 and (stop - start) % BODY == 0:
                with eng.Fori(0, n) as it:
                    for k in range(BODY):
                        body(it * BODY + (start + k), start + k)
            else:
                for i in range(start, stop):
                    body(i, i)

        def slot_row(slot, r):
            return slot * J + (1 if r >= SPILL else 0)

        def xin_rows(b, k0, k1):
            return slice(b * J + k0, b * J + k1)

        def image_of(q, r):
            return q if r < SPILL else q + SPILL if r < RES else q - RES + SPILL

        third = (J - 1) // 3
        cut = 1 + 2 * third

        flat = lambda ap: ap.rearrange("p k w -> p (k w)")[:, 0:PIX]
        split_f32 = split[:, :, :, :, :].rearrange("p a b k w -> p (a b k w)").bitcast(F32)
        own_buffers = [flat(xin[:, xin_rows(b, 0, J)]) for b in range(4)] + [
            spare[:, :], spare2[:, :], first_only[:, :], flat(act[:, 0]), flat(act[:, 1]), split_f32[:, 0:PIX],
            flat(stage[:, 0]), split_f32[:, KB * W:KB * W + PIX], flat(stage[:, 1])]
        EARLY = 7
        OWN = len(own_buffers)
        assert OWN == len(x3_own_loaded)

        def first_use(b):
            return OWN + (b - OWN) % 4

        def place(q, r):
            return slots_sb[:, bass.ds(slot_row(q if r < RES else q - RES, r % RES), J), :]

        def x3_buffer(r):
            return own_buffers[r if r < OWN else r % 4]

        PADS_W, PADS_0, PADS_1 = 1, 4, 7
        MASKS = 4

        block = ctx.enter_context(nc.Block())

        @block.sync
        def _(sp):
            def load_x(j, r):
                b = r % 4
                if r >= 4:
                    sp.wait_ge(act_ready[0], j - 3)
                    if r - 4 < DIRECT[0]:
                        sp.wait_ge(half_lo[0], j - 3)
                src = odd_even(x[j])
                if r == 0:
                    sp.dma_start(xin[0:C, 1:cut, :], src[1][:, 0:cut - 1, :]).then_inc(x0_first_rows, 16)
                    sp.dma_start(xin[C:P, 0:cut, :], src[0][:, 0:cut, :]).then_inc(x0_first_rows, 16)
                    sp.dma_start(xin[0:C, cut:KB, :], src[1][:, cut - 1:J, :]).then_inc(x_loaded[b], 16)
                    sp.dma_start(xin[C:P, cut:J, :], src[0][:, cut:J, :]).then_inc(x_loaded[b], 16)
                    return
                sp.dma_start(xin[0:C, xin_rows(b, 1, KB), :], src[1]).then_inc(x_loaded[b], 16)
                sp.dma_start(xin[C:P, xin_rows(b, 0, J), :], src[0]).then_inc(x_loaded[b], 16)

            for h in range(2):
                sp.dma_start(wraw[C * h:C * h + C, :], w1.rearrange("o i a b -> o (i a b)")).then_inc(weights_loaded[0], 16)
            for j in range(3):
                load_x(j, j)
            for col, v in enumerate((b1, g1, be1, b2, g2, be2)):
                for h in range(2):
                    sp.dma_start(par[C * h:C * h + C, col:col + 1], v.rearrange("(c a) -> c a", a=1)).then_inc(params_loaded, 16)
            load_x(3, 3)
            load_x(4, 4)
            sp.wait_ge(quantised, 1)
            for h in range(2):
                sp.dma_start(wraw[C * h:C * h + C, :], w2.rearrange("o i a b -> o (i a b)")).then_inc(weights_loaded[1], 16)

            def pass1(i, r):
                if r + 5 < NIMG:
                    load_x(i + 5, r + 5)
                b = r % 2
                sp.wait_ge(pair_evac[0][1], i + 1)
                done = stage_stored[0][b]
                if r < SPILL:
                    for h in range(2):
                        sp.dma_start(y1_spill[i, C * h:C * h + C, :],
                                     stage[C * h:C * h + C, b].rearrange("p j w -> p (j w)")).then_inc(done, 16)
                else:
                    base = slot_row(i - SPILL, r - SPILL)
                    sp.dma_start(slots_sb[0:C, bass.ds(base + 1, J), :], stage[C:P, b]).then_inc(done, 16)
                    sp.dma_start(slots_sb[C:P, bass.ds(base, J), :], stage[0:C, b]).then_inc(done, 16)

            run_slots(sp, 0, BODY, pass1)
            run_slots(sp, BODY, SPILL, pass1)
            run_slots(sp, SPILL, NIMG - 2 * BODY, pass1)
            run_slots(sp, NIMG - 2 * BODY, NIMG - BODY, pass1)
            run_slots(sp, NIMG - BODY, NIMG, pass1)
            for b in range(2):
                sp.wait_ge(stage_stored[0][b], 16 * NIMG)

            def load_y1(p, r):
                b = r % 4
                base = slot_row(p - RES, r - RES)
                img = p - RES
                sp.dma_start(slots_sb[0:C, bass.ds(base + 1, J), :],
                             y1_spill[img, C:P, :].rearrange("p (j w) -> p j w", w=W)).then_inc(y1_loaded[b], 16)
                sp.dma_start(slots_sb[C:P, bass.ds(base, J), :],
                             y1_spill[img, 0:C, :].rearrange("p (j w) -> p j w", w=W)).then_inc(y1_loaded[b], 16)

            def load_x3(q, r, img):
                if r >= OWN + 4:
                    sp.wait_ge(out_ready, q - 3)
                elif r >= OWN:
                    sp.wait_ge(out_ready, r % 4 + 1)
                buf = x3_buffer(r).rearrange("p (j w) -> p j w", w=W)
                loaded = x3_own_loaded[r] if r < OWN else x3_loaded[r % 4]
                src = x[img].rearrange("c (h r) w -> h c r w", h=2)
                for h in range(2):
                    sp.dma_start(buf[C * h:C * h + C], src[h]).then_inc(loaded, 16)

            def pass2(i, r):
                if RES <= r + 4 < NIMG:
                    sp.wait_ge(act_ready[1], i + 1)
                    load_y1(i + 4, r + 4)
                n = r - (SPILL - BODY)
                if 0 <= n < EARLY:
                    load_x3(n, n, n)
                b = r % 2
                sp.wait_ge(pair_evac[1][1], i + 1)
                done = stage_stored[1][b]
                if r < SPILL:
                    dst = odd_even(y2_spill[i])
                    for h in range(2):
                        for part in range(2):
                            sp.dma_start(dst[h][:, part * J // 2:(part + 1) * J // 2, :],
                                         stage[C * h:C * h + C, b, part * J // 2:(part + 1) * J // 2]).then_inc(done, 16)
                else:
                    base = slot_row(i if r < RES else i - RES, r % RES)
                    for h in range(2):
                        for part in range(2):
                            sp.dma_start(
                                slots_sb[C * part:C * part + C, bass.ds(base + h, J // 2, 2), :],
                                stage[C * h:C * h + C, b, part * J // 2:(part + 1) * J // 2]).then_inc(done, 16)

            run_slots(sp, 0, SPILL - BODY, pass2)
            run_slots(sp, SPILL - BODY, SPILL, pass2)
            run_slots(sp, SPILL, RES - BODY, pass2)
            run_slots(sp, RES - BODY, RES, pass2)
            run_slots(sp, RES, NIMG - BODY, pass2)
            run_slots(sp, NIMG - BODY, NIMG - 3, pass2)
            sp.wait_ge(lo_ready[1], NIMG - 1)
            load_x3(7, 7, 7)
            run_slots(sp, NIMG - 3, NIMG - 2, pass2)
            sp.wait_ge(lo_ready[1], NIMG)
            load_x3(8, 8, 8)
            run_slots(sp, NIMG - 2, NIMG - 1, pass2)
            sp.wait_ge(pair_done[1][1], NIMG - 1)
            load_x3(9, 9, 9)
            sp.wait_ge(stage_stored[1][0], 32 * NIMG)
            sp.wait_ge(stage_read[1], NIMG - 1)
            load_x3(10, 10, 10)
            run_slots(sp, NIMG - 1, NIMG, pass2)
            sp.wait_ge(pair_done[1][1], NIMG)
            load_x3(11, 11, 11)
            sp.wait_ge(stage_stored[1][1], 32 * NIMG)
            sp.wait_ge(stage_read[1], NIMG)
            load_x3(12, 12, image_of(12, 12))

            def load_y2(m, r):
                if r == 0:
                    sp.wait_ge(half_stored, 32)
                sp.wait_ge(out_stored[r % 4], (m - r % 4) * 8 + 32)
                for h in range(2):
                    sp.dma_start(slots_sb[C * h:C * h + C, bass.ds(slot_row(m, r), J), :],
                                 y2_spill[m].rearrange("c (h r) w -> h c r w", h=2)[h]).then_inc(y2_loaded[r % 4], 16)

            def pass3(q, r):
                if r == 0:
                    sp.wait_ge(half_out, 1)
                    for h in range(2):
                        sp.dma_start(out[image_of(0, 0)].rearrange("c (h r) w -> h c r w", h=2)[h][:, 0:J // 2, :],
                                     place(0, 0)[C * h:C * h + C, 0:J // 2]).then_inc(half_stored, 16)
                    rows = slice(J // 2, J)
                else:
                    rows = slice(0, J)
                sp.wait_ge(out_ready, q + 1)
                dst = out[image_of(q, r)]
                dst = dst.rearrange("c (h r) w -> h c r w", h=2)
                result = place(q, r)
                for h in range(2):
                    sp.dma_start(dst[h][:, rows, :], result[C * h:C * h + C, rows]).then_inc(out_stored[r % 4], 16)
                if r < 4:
                    n = first_use(q)
                    load_x3(n, n, image_of(n, n))
                elif OWN <= r < NIMG - 4:
                    load_x3(q + 4, r + 4, image_of(q + 4, r + 4))
                if 2 <= r < SPILL + 2:
                    load_y2(q - 2, r - 2)

            for start, stop in ((0, SPILL), (SPILL, RES - 4), (RES - 4, RES), (RES, NIMG - 4), (NIMG - 4, NIMG)):
                for first in ([start] if start else [0, 4, 8]):
                    run_slots(sp, first, stop if start else first + 4, pass3)
            for b in range(4):
                sp.wait_ge(out_stored[b], 8 * NIMG)

        @block.gpsimd
        def _(pool):
            nc.gpsimd.memset(ident[:, :], 0.0).then_inc(masks_zeroed, 1)
            nc.gpsimd.memset(same_channel[:, :], 0.0).then_inc(masks_zeroed, 1)
            made = zeroed = reduced = 0

            def cores_together():
                for semaphore, count in ((pads_zeroed, zeroed), (masks_made, made), (absmax_all, reduced)):
                    if count:
                        pool.wait_ge(semaphore, count)

            def zero(*paddings):
                nonlocal zeroed
                for padding in paddings:
                    cores_together()
                    nc.gpsimd.memset(padding, 0.0).then_inc(pads_zeroed, 1)
                    zeroed += 1

            def diagonal(m, pattern, base, fill):
                nonlocal made
                cores_together()
                nc.gpsimd.affine_select(out=m, in_=m, compare_op=ALU.not_equal, fill=fill, base=base,
                                        pattern=pattern, channel_multiplier=1).then_inc(masks_made, 1)
                made += 1

            def largest(n):
                nonlocal reduced
                cores_together()
                pool.wait_ge(absmax_ready, n + 1)
                nc.gpsimd.partition_all_reduce(wstat[:, n + 2:n + 3], wstat[:, n:n + 1], P,
                                               bass.bass_isa.ReduceOp.max).then_inc(absmax_all, 1)
                reduced += 1

            zero(wpad[:, :, 0:5:4, :])
            pool.wait_ge(masks_zeroed, 2)
            diagonal(ident[:, :], [[-1, C]], 0, 1.0)
            for other_half in (0, C, -C):
                diagonal(same_channel[:, :], [[-1, P]], other_half, 0.5 / GRP)
            assert made == MASKS
            largest(0)
            for n in range(2):
                zero(act[0:C, n, 0, :], act[C:P, n, KB - 1, :],
                     hi[0:C, n, 0, :])
                assert zeroed == (PADS_0, PADS_1)[n]
            largest(1)

        @block.scalar
        def _(sc):
            def split_hi(ph, i, r):
                k = r % 2
                sc.wait_ge(act_ready[ph], i + 1)
                if r >= 2:
                    sc.wait_ge(pair_done[ph][1], i - 1)
                nc.scalar.copy(hi[:, k, :], act[:, k]).then_inc(hi_ready[ph], 1)

            def normalise(ph, i, r, rows, func, scale, bias):
                k = r % 2
                if r >= 2:
                    sc.wait_ge(lo_ready[ph], i - 1)
                nc.scalar.activation(act[:, k, 1:J, :], rows(0, P, 1, J), func, bias=bias(0, P), scale=scale(0, P))
                nc.scalar.activation(act[C:P, k, 0, :], rows(C, P, 0, 1), func, bias=bias(C, P), scale=scale(C, P))
                nc.scalar.activation(act[0:C, k, J, :], rows(0, C, J, KB), func, bias=bias(0, C),
                                     scale=scale(0, C)).then_inc(act_ready[ph], 1)

            def halves(ph, i, func, rows, scale, bias):
                k = i % 2
                if i >= 2:
                    sc.wait_ge(pair_done[ph][1], i - 1)
                nc.scalar.activation(hi[C:P, k, 0], rows(C, P, 0, 1), func, bias=bias(C, P), scale=scale(C, P))
                nc.scalar.activation(hi[:, k, 1:HALF], rows(0, P, 1, HALF), func, bias=bias(0, P),
                                     scale=scale(0, P)).then_inc(half_hi[ph], 1)
                if i >= 2:
                    sc.wait_ge(lo_ready[ph], i - 1)
                nc.scalar.activation(act[:, k, HALF:J, :], rows(0, P, HALF, J), func, bias=bias(0, P), scale=scale(0, P))
                nc.scalar.activation(act[0:C, k, J, :], rows(0, C, J, KB), func, bias=bias(0, C),
                                     scale=scale(0, C)).then_inc(act_ready[ph], 1)
                sc.wait_ge(act_ready[ph], i + 1)
                nc.scalar.copy(hi[:, k, HALF:KB], act[:, k, HALF:KB]).then_inc(hi_ready[ph], 1)

            def x_args(i, r):
                def rows(a, b, k0, k1):
                    ap = xin[a:b, xin_rows(r % 4, k0, k1), :]
                    return ap.rearrange("p k w -> p (k w)") if k1 - k0 == 1 else ap
                return rows, lambda a, b: gn_s_all[a:b, bass.ds(i, 1)], lambda a, b: gn_b_all[a:b, bass.ds(i, 1)]

            def halves_x(i):
                sc.wait_ge(gn_coef_ready, i + 1 if i < ALONE else i + 2 - i % 2)
                rows, scale, bias = x_args(i, i)
                halves(0, i, ACT.Identity, rows, scale, bias)

            def normalise_x(i, r):
                sc.wait_ge(gn_coef_ready, i + 2 - r % 2)
                rows, scale, bias = x_args(i, r)
                normalise(0, i, r, rows, ACT.Identity, scale, bias)

            def halves_y1():
                sc.wait_ge(stage_stored[0][0], 16 * SPILL + 32)
                halves(1, 0, ACT.Relu, lambda a, b, k0, k1: slots_sb[a:b, k0:k1, :],
                       lambda a, b: A1[a:b, :], lambda a, b: B1[a:b, :])

            def normalise_y1(i, r):
                if r >= RES:
                    sc.wait_ge(y1_loaded[r % 4], i * 8 + (32 - 8 * (r % 4) - 8 * RES))
                else:
                    sc.wait_ge(stage_stored[0][r % 2], (i - r % 2) * 16 + (16 * SPILL + 32))
                base = slot_row(i if r < RES else i - RES, r % RES)
                normalise(1, i, r, lambda a, b, k0, k1: slots_sb[a:b, bass.ds(base + k0, k1 - k0), :],
                          ACT.Relu, lambda a, b: A1[a:b, :], lambda a, b: B1[a:b, :])

            def evacuate(ph, i, r, p):
                b = r % 2
                if p == 0 and r >= 2:
                    sc.wait_ge(stage_stored[ph][b], (i - b) * (16 if ph == 0 else 32))
                    sc.wait_ge(stage_read[ph], i - 1)
                if p == 0 and r < 2 and ph == 1:
                    sc.wait_ge(stage_stored[0][b], 16 * NIMG)
                if r == NIMG - 1 and p == 1:
                    for c, done, evacuated, count in ((2, chunk_done[ph], chunk_evac[ph], 1),
                                                      (3, pair_done[ph][1], pair_evac[ph][1], NIMG)):
                        sc.wait_ge(done, count)
                        nc.scalar.activation(
                            stage[:, b, c * ROWS_PER_BANK:(c + 1) * ROWS_PER_BANK, :].rearrange("q j w -> q (j w)"),
                            conv_ps[:, c, 0:CH], ACT.Identity, bias=par[:, 3 * ph:3 * ph + 1],
                            scale=evac_scale[:, ph:ph + 1]).then_inc(evacuated, 1)
                    return
                sc.wait_ge(pair_done[ph][p], i + 1)
                rows = 2 * ROWS_PER_BANK
                nc.scalar.activation(
                    stage[:, b, p * rows:(p + 1) * rows, :].rearrange("q (n j) w -> q n (j w)", n=2),
                    conv_ps[:, 2 * p:2 * p + 2, 0:CH], ACT.Identity, bias=par[:, 3 * ph:3 * ph + 1],
                    scale=evac_scale[:, ph:ph + 1]).then_inc(pair_evac[ph][p], 1)

            def gn_sqrt(i, r):
                m = r % 2
                sc.wait_ge(gn_var_ready, i + 1)
                nc.scalar.activation(gn_sd[:, m:m + 1], gn_var[:, m:m + 1], ACT.Sqrt, scale=-1.0).then_inc(gn_sd_ready, 1)

            def gn_pair_sqrt(i):
                sc.wait_ge(gn_var_ready, i + 2)
                nc.scalar.activation(gn_sd[:, :], gn_var[:, :], ACT.Sqrt).then_inc(gn_sd_ready, 2)

            def pass1(i, r):
                evacuate(0, i - 1, r - 1, 1)
                if r + 1 < NIMG:
                    normalise_x(i + 1, r + 1)
                    split_hi(0, i + 1, r + 1)
                    if r % 2 == 0 and r + 2 < NIMG:
                        gn_pair_sqrt(i + 2)
                if r < NIMG:
                    evacuate(0, i, r, 0)

            sc.wait_ge(pads_zeroed, PADS_W)
            nc.scalar.activation(warm[:, :], wpad[:, 0, 0, 0:1], ACT.Sqrt)
            sc.wait_ge(transposed, 1)
            nc.scalar.copy(wmat[0][:, :, :, :], wt_ps[0][:, :, :, :]).then_inc(wmat_ready, 1)
            gn_sqrt(0, 0)
            sc.wait_ge(pads_zeroed, PADS_0)
            halves_x(0)
            gn_sqrt(1, 1)
            sc.wait_ge(pads_zeroed, PADS_1)
            sc.wait_ge(params_loaded, 12 * 16)
            sc.wait_ge(evac_scale_ready, 1)
            evacuate(0, 0, 0, 0)
            halves_x(1)
            evacuate(0, 0, 0, 1)
            gn_sqrt(2, 2)
            halves_x(2)
            evacuate(0, 1, 1, 0)
            evacuate(0, 1, 1, 1)
            gn_sqrt(3, 3)
            halves_x(3)
            evacuate(0, 2, 2, 0)
            evacuate(0, 2, 2, 1)
            gn_pair_sqrt(4)
            halves_x(4)
            evacuate(0, 3, 3, 0)
            run_slots(sc, BODY, NIMG - BODY, pass1)
            run_slots(sc, NIMG - BODY, NIMG + 1, pass1)

            def bn_sqrt(ph):
                sc.wait_ge(bn_var_ready[ph], 1)
                nc.scalar.activation(bn_sd[:, ph:ph + 1], bn_w[:, ph, 3:4], ACT.Sqrt, scale=-1.0).then_inc(bn_sd_ready[ph], 1)

            bn_sqrt(0)
            sc.wait_ge(bn_coef_ready[0], 1)
            sc.wait_ge(evac_scale_ready, 2)

            def pass2(i, r):
                if r + 1 < NIMG and r >= 0:
                    split_hi(1, i + 1, r + 1)
                if r + 2 < NIMG:
                    normalise_y1(i + 2, r + 2)
                if r >= 0:
                    evacuate(1, i, r, 0)
                    evacuate(1, i, r, 1)

            halves_y1()
            run_slots(sc, -1, 2, pass2)
            run_slots(sc, 2, SPILL - 2, pass2)
            run_slots(sc, SPILL - 2, RES - 2, pass2)
            run_slots(sc, RES - 2, NIMG - 2, pass2)
            run_slots(sc, NIMG - 2, NIMG, pass2)
            bn_sqrt(1)
            sc.wait_ge(skip_coef, 3)

            def pass3(q, r):
                if r >= RES:
                    sc.wait_ge(y2_loaded[r % 4], q * 8 + (32 - 8 * (r % 4) - 8 * RES))
                if r < SPILL:
                    sc.wait_ge(stage_stored[1][r % 2], (q - r % 2) * 32 + (32 * RES + 64))
                slot = place(q, r)
                img = image_of(q, r)
                for rows, ready in (((slice(0, J // 2), half_u), (slice(J // 2, J), u_ready)) if r == 0 else
                                    ((slice(0, J), u_ready),)):
                    nc.scalar.activation(slot[:, rows], slot[:, rows], ACT.Identity,
                                         bias=skip_b[:, bass.ds(img, 1)], scale=A2).then_inc(ready, 1)

            run_slots(sc, 0, BODY, pass3)
            run_slots(sc, BODY, SPILL, pass3)
            run_slots(sc, SPILL, RES, pass3)
            run_slots(sc, RES, NIMG, pass3)

        @block.vector
        def _(dve):
            steps = 0

            def setup_step(ins):
                nonlocal steps
                steps += 1
                ins.then_inc(wprep, 1)
                dve.wait_ge(wprep, steps)

            def weight_absmax(n):
                dve.wait_ge(weights_loaded[n], 32)
                nc.vector.tensor_reduce(wstat[:, n:n + 1], wraw[:, :], AX.X, ALU.max,
                                        apply_absolute_value=True).then_inc(absmax_ready, 1)

            def quantise(n):
                dve.wait_ge(absmax_all, n + 1)
                setup_step(nc.vector.tensor_scalar(qscale[:, n:n + 1], wstat[:, n + 2:n + 3], 1.0 / QMAX, None, ALU.mult))
                setup_step(nc.vector.reciprocal(wstat[:, n + 4:n + 5], qscale[:, n:n + 1]))
                setup_step(nc.vector.tensor_scalar(wraw[0:C, :], wraw[0:C, :], wstat[0:C, n + 4:n + 5], ROUND,
                                                   ALU.mult, ALU.add))
                dve.wait_ge(pads_zeroed, PADS_W)
                nc.vector.tensor_scalar(
                    wpad[:, :, 1:4, :].rearrange("o kx ky i -> o i ky kx"),
                    wraw[0:C, :].rearrange("o (i ky kx) -> o i ky kx", ky=3, kx=3), ROUND, None,
                    ALU.subtract).then_inc(quantised, 1)
                nc.vector.tensor_scalar(evac_scale[:, n:n + 1], qscale[:, n:n + 1],
                                        1.0 / (GN_SCALE, BN_SCALE)[n], None, ALU.mult).then_inc(evac_scale_ready, 1)

            def power_of_two():
                dve.wait_ge(params_loaded, 12 * 16)
                setup_step(nc.vector.tensor_reduce(pabs[:, 0:1], par[:, 1:3], AX.X, ALU.add, apply_absolute_value=True))
                setup_step(nc.vector.tensor_scalar(pabs[:, 1:2].bitcast(U32), pabs[:, 0:1].bitcast(U32), 0x7F800000, None,
                                                   ALU.bitwise_and))
                setup_step(nc.vector.tensor_scalar(pow2[:, 0:1], pabs[:, 1:2], 2.0 ** -60, None, ALU.max))
                setup_step(nc.vector.reciprocal(pabs[:, 0:1], pow2[:, 0:1]))
                setup_step(nc.vector.tensor_scalar(pow2[:, 1:2], pabs[:, 0:1], BN_SCALE, None, ALU.mult))
                setup_step(nc.vector.tensor_scalar(bn_affine[:, 0, 0:1], par[:, 1:2], 0.5, pow2[:, 1:2], ALU.mult, ALU.mult))
                setup_step(nc.vector.tensor_scalar(bn_affine[:, 0, 1:2], par[:, 2:3], pow2[:, 1:2], None, ALU.mult))
                setup_step(nc.vector.tensor_scalar(bn_affine[:, 1, 0:1], par[:, 4:5], 0.5, None, ALU.mult))
                setup_step(nc.vector.tensor_copy(bn_affine[:, 1, 1:2], par[:, 5:6]))

            def averages():
                dve.wait_ge(masks_made, MASKS)
                pairs = same_channel[:, :].rearrange("p (g e) -> p g e", e=GRP)
                for e in range(GRP):
                    ins = nc.vector.tensor_tensor(gn_avg[:, :].rearrange("p (g e) -> p g e", e=GRP)[:, :, e],
                                                  pairs[:, :, 0], pairs[:, :, 1], ALU.add)
                ins.then_inc(averages_made, 1)

            def bn_average():
                nc.vector.tensor_scalar(bn_avg[:, :], same_channel[:, :], GRP * BODY / NIMG, None,
                                        ALU.mult).then_inc(averages_made, 1)

            def conv2_matrix():
                dve.wait_ge(transposed, 2)
                nc.vector.tensor_scalar(wmat[1][:, :, :, :], wt_ps[1][:, :, :, :], pow2[:, 0:1], None,
                                        ALU.mult).then_inc(wmat_ready, 1)

            def gn_stats(i, r, parts=(0, 1, 2, 3)):
                b, m = r % 4, r % 2
                if parts[0] == 0:
                    if r == 0:
                        dve.wait_ge(x0_first_rows, 32)
                    else:
                        dve.wait_ge(x_loaded[b], i * 8 + (32 - 8 * b))
                    if r >= 2:
                        dve.wait_ge(gn_moments, i - 1)
                for t in parts:
                    if r == 0 and t == 2:
                        dve.wait_ge(x_loaded[b], 32)
                    if t < 3:
                        nc.vector.bn_stats(gn_tup[:, m, t, :],
                                           xin[:, xin_rows(b, 1 + t * third, 1 + (t + 1) * third), :].rearrange("p k w -> p (k w)"))
                    else:
                        nc.vector.bn_stats(gn_tup[C:P, m, 3, :], xin[C:P, b * J, :])
                        nc.vector.bn_stats(gn_tup[0:C, m, 3, :], xin[0:C, b * J + J, :]).then_inc(gn_tuples, 1)

            def chain(semaphore, base):
                n = 0

                def step(ins, count=1):
                    nonlocal n
                    n += count
                    ins.then_inc(semaphore, count)
                    dve.wait_ge(semaphore, base + n)
                return step

            B1_STEPS, B_STEPS = 2, 5

            def gn_chain_a(i, r):
                m = r % 2
                mean, second = gn_mv[:, m, 0:1], gn_mv[:, m, 1:2]
                dve.wait_ge(gn_tuples, i + 1)
                if r >= 2:
                    dve.wait_ge(gn_combined, i - 1)
                nc.vector.memset(gn_sq[:, m:m + 1], 0.0)
                nc.vector.bn_aggr(gn_mv[:, m, :], gn_tup[:, m].rearrange("p a b -> p (a b)")).then_inc(gn_step_a, 1)
                dve.wait_ge(gn_step_a, i + 1)
                nc.vector.scalar_tensor_tensor(out=second, in0=mean, scalar=mean, in1=second,
                                               op0=ALU.mult, op1=ALU.add).then_inc(gn_moments, 1)

            def gn_chain_b1(i, r):
                m = r % 2
                mean = gn_g[:, m, 0:1]
                step = chain(gn_step_b, i * B_STEPS)
                dve.wait_ge(gn_combined, i + 1)
                step(nc.vector.tensor_copy(gn_g[:, m, :], stat_ps[:, 2 * m:2 * m + 2]))
                step(nc.vector.scalar_tensor_tensor(out=gn_tmp[:, 0, m:m + 1], in0=mean, scalar=mean,
                                                    in1=gn_g[:, m, 1:2], op0=ALU.mult, op1=ALU.subtract))
                nc.vector.tensor_scalar(gn_var[:, m:m + 1], gn_tmp[:, 0, m:m + 1], 0.0, GN_EPS, ALU.min,
                                        ALU.subtract).then_inc(gn_var_ready, 1)

            def gn_chain_b2(i, r):
                m = r % 2
                root, correction, scale = gn_tmp[:, 2, m:m + 1], gn_tmp[:, 1, m:m + 1], gn_s_all[:, bass.ds(i, 1)]
                step = chain(gn_step_b, i * B_STEPS + B1_STEPS)
                dve.wait_ge(gn_sd_ready, i + 1)
                step(nc.vector.reciprocal(root, gn_sd[:, m:m + 1]))
                step(nc.vector.scalar_tensor_tensor(out=correction, in0=root, scalar=root, in1=gn_var[:, m:m + 1],
                                                    op0=ALU.mult, op1=ALU.mult))
                step(nc.vector.tensor_scalar(gn_tmp[:, 3, m:m + 1], correction, 0.5 * GN_SCALE, 1.5 * GN_SCALE,
                                             ALU.mult, ALU.add))
                nc.vector.tensor_tensor(scale, gn_tmp[:, 3, m:m + 1], root, ALU.mult).then_inc(gn_scale_ready, 1)
                dve.wait_ge(gn_scale_ready, i + 1)
                nc.vector.scalar_tensor_tensor(out=gn_b_all[:, bass.ds(i, 1)], in0=gn_g[:, m, 0:1], scalar=-1.0, in1=scale,
                                               op0=ALU.mult, op1=ALU.mult).then_inc(gn_coef_ready, 1)

            def gn_pair_a(i, r):
                dve.wait_ge(gn_tuples, i + 2)
                dve.wait_ge(gn_combined, i)
                nc.vector.memset(gn_sq[:, :], 0.0)
                for m in range(2):
                    ins = nc.vector.bn_aggr(gn_mv[:, m, :], gn_tup[:, m].rearrange("p a b -> p (a b)"))
                ins.then_inc(gn_step_a, 1)
                dve.wait_ge(gn_step_a, i + 1)
                nc.vector.tensor_tensor(gn_sq[:, :], gn_mv[:, :, 0], gn_mv[:, :, 0], ALU.mult).then_inc(gn_step_a, 1)
                dve.wait_ge(gn_step_a, i + 2)
                nc.vector.tensor_tensor(gn_mv[:, :, 1], gn_mv[:, :, 1], gn_sq[:, :], ALU.add).then_inc(gn_moments, 2)

            PAIR_STEPS = 8

            def pair_base(i):
                return i * (PAIR_STEPS // 2) + ALONE * (B_STEPS - PAIR_STEPS // 2)

            def gn_pair_b1(i, r):
                step = chain(gn_step_b, pair_base(i))
                dve.wait_ge(gn_combined, i + 2)
                step(nc.vector.tensor_copy(gn_g[:, :, :].rearrange("p a b -> p (a b)"), stat_ps[:, 0:4]))
                step(nc.vector.tensor_tensor(gn_tmp[:, 0, :], gn_g[:, :, 0], gn_g[:, :, 0], ALU.mult))
                step(nc.vector.tensor_tensor(gn_tmp[:, 1, :], gn_g[:, :, 1], gn_tmp[:, 0, :], ALU.subtract))
                nc.vector.tensor_scalar(gn_var[:, :], gn_tmp[:, 1, :], 0.0, GN_EPS, ALU.max, ALU.add).then_inc(gn_var_ready, 2)

            def gn_pair_b2(i, r):
                scale = gn_s_all[:, bass.ds(i, 2)]
                step = chain(gn_step_b, pair_base(i) + 3)
                dve.wait_ge(gn_sd_ready, i + 2)
                step(nc.vector.reciprocal(gn_tmp[:, 2, :], gn_sd[:, :]))
                step(nc.vector.tensor_tensor(gn_tmp[:, 0, :], gn_tmp[:, 2, :], gn_tmp[:, 2, :], ALU.mult))
                step(nc.vector.tensor_tensor(gn_tmp[:, 1, :], gn_tmp[:, 0, :], gn_var[:, :], ALU.mult))
                step(nc.vector.tensor_scalar(gn_tmp[:, 3, :], gn_tmp[:, 1, :], -0.5 * GN_SCALE, 1.5 * GN_SCALE,
                                             ALU.mult, ALU.add), count=2)
                nc.vector.tensor_tensor(scale, gn_tmp[:, 3, :], gn_tmp[:, 2, :], ALU.mult).then_inc(gn_scale_ready, 2)
                dve.wait_ge(gn_scale_ready, i + 2)
                nc.vector.scalar_tensor_tensor(out=gn_b_all[:, bass.ds(i, 2)], in0=gn_g[:, :, 0], scalar=-1.0, in1=scale,
                                               op0=ALU.mult, op1=ALU.mult).then_inc(gn_coef_ready, 2)

            def half_act_x(i):
                k = i % 2
                dve.wait_ge(gn_coef_ready, i + 1 if i < ALONE else i + 2)
                for a, b, k0, k1 in ((C, P, 0, 1), (0, P, 1, HALF)):
                    ins = nc.vector.tensor_scalar(act[a:b, k, k0:k1, :], xin[a:b, xin_rows(i % 4, k0, k1), :],
                                                  gn_s_all[a:b, i:i + 1], gn_b_all[a:b, i:i + 1], ALU.mult, ALU.add)
                ins.then_inc(half_act[0], 1)

            def half_lo_x(i):
                k = i % 2
                dve.wait_ge(half_act[0], i + 1)
                dve.wait_ge(half_hi[0], i + 1)
                nc.vector.tensor_tensor(lo[:, k, 0:HALF], act[:, k, 0:HALF], hi[:, k, 0:HALF],
                                        ALU.subtract).then_inc(half_lo[0], 1)

            def half_lo_y1():
                for a, b, k0, k1 in ((C, P, 0, 1), (0, P, 1, HALF)):
                    ins = nc.vector.tensor_scalar(act[a:b, 0, k0:k1, :], slots_sb[a:b, k0:k1, :], A1[a:b, :], B1[a:b, :],
                                                  ALU.mult, ALU.add)
                ins.then_inc(half_act[1], 1)
                dve.wait_ge(half_act[1], 1)
                dve.wait_ge(half_hi[1], 1)
                nc.vector.scalar_tensor_tensor(out=lo[:, 0, 0:HALF], in0=act[:, 0, 0:HALF], scalar=0.0,
                                               in1=hi[:, 0, 0:HALF], op0=ALU.max,
                                               op1=ALU.subtract).then_inc(half_lo[1], 1)

            def rest_lo(ph, i):
                dve.wait_ge(hi_ready[ph], i + 1)
                nc.vector.tensor_tensor(lo[:, i % 2, HALF:KB], act[:, i % 2, HALF:KB], hi[:, i % 2, HALF:KB],
                                        ALU.subtract).then_inc(lo_ready[ph], 1)

            def split_lo(ph, i, r):
                k = r % 2
                dve.wait_ge(hi_ready[ph], i + 1)
                nc.vector.tensor_tensor(lo[:, k, :], act[:, k], hi[:, k, :], ALU.subtract).then_inc(lo_ready[ph], 1)

            def bn_stats(ph, i, r, p, chunks=(0, 1)):
                by_chunk = r == NIMG - 1 and p == 1
                if by_chunk:
                    dve.wait_ge(chunk_evac[ph], 1)
                else:
                    dve.wait_ge(pair_evac[ph][p], i + 1)
                if r % BODY == 0 and p == 0 and r >= BODY:
                    dve.wait_ge(bn_sums[ph], i)
                rows = ROWS_PER_BANK
                for n in chunks:
                    c = 2 * p + n
                    if by_chunk and n == 1:
                        dve.wait_ge(pair_evac[ph][p], NIMG)
                    ins = nc.vector.bn_stats(bn_tup[:, (r % BODY) * NCH + c, :],
                                             stage[:, r % 2, c * rows:(c + 1) * rows, :].rearrange("q j w -> q (j w)"))
                if c == NCH - 1:
                    ins.then_inc(stage_read[ph], 1)

            def bn_accumulate(ph, i, r):
                base = i - (BODY - 1)
                mean, second = bn_mv[:, 0:1], bn_mv[:, 1:2]
                dve.wait_ge(stage_read[ph], i + 1)
                nc.vector.memset(bn_sq[:, :], 0.0)
                nc.vector.bn_aggr(bn_mv[:, :], bn_tup[:, :, :].rearrange("p a b -> p (a b)")).then_inc(bn_step[ph], BODY // 2)
                dve.wait_ge(bn_step[ph], base + BODY // 2)
                nc.vector.scalar_tensor_tensor(out=second, in0=mean, scalar=mean, in1=second, op0=ALU.mult,
                                               op1=ALU.add).then_inc(bn_step[ph], BODY // 2)
                dve.wait_ge(bn_step[ph], base + BODY)
                nc.vector.tensor_tensor(bn_acc[ph][:, :], bn_acc[ph][:, :], bn_mv[:, :], ALU.add).then_inc(bn_sums[ph], BODY)

            def bn_coefficients(ph):
                step = chain(bn_chain[ph], 0)
                v = lambda c: bn_w[:, ph, c:c + 1]
                mean, neg_mean, neg_var, root = v(0), v(4), v(3), v(5)
                half_gamma, beta = bn_affine[:, ph, 0:1], bn_affine[:, ph, 1:2]
                dve.wait_ge(bn_combined[ph], 1)
                step(nc.vector.tensor_copy(bn_w[:, ph, 0:2], stat_ps[:, 0:2]))
                step(nc.vector.scalar_tensor_tensor(out=v(2), in0=mean, scalar=mean, in1=v(1), op0=ALU.mult, op1=ALU.subtract))
                nc.vector.tensor_scalar(neg_var, v(2), 0.0, BN_EPS, ALU.min, ALU.subtract).then_inc(bn_var_ready[ph], 1)
                step(nc.vector.tensor_scalar(neg_mean, mean, -1.0, None, ALU.mult))
                dve.wait_ge(bn_sd_ready[ph], 1)
                step(nc.vector.reciprocal(root, bn_sd[:, ph:ph + 1]))
                nc.vector.tensor_tensor(v(7), root, half_gamma, ALU.mult)
                step(nc.vector.scalar_tensor_tensor(out=v(6), in0=root, scalar=root, in1=neg_var, op0=ALU.mult, op1=ALU.mult))
                step(nc.vector.scalar_tensor_tensor(out=v(8), in0=v(6), scalar=3.0, in1=v(7), op0=ALU.add, op1=ALU.mult))
                shift = nc.vector.scalar_tensor_tensor(out=v(9), in0=v(8), scalar=neg_mean, in1=beta, op0=ALU.mult, op1=ALU.add)
                if ph == 0:
                    shift.then_inc(bn_coef_ready[0], 1)
                else:
                    step(shift)
                    nc.vector.tensor_scalar(skip_b[:, :], gn_b_all[:, :], v(9), None, ALU.add).then_inc(skip_coef, 1)

            def skip_coefficients():
                nc.vector.tensor_scalar(skip_s[:, :], gn_s_all[:, :], 1.0 / GN_SCALE, None, ALU.mult).then_inc(skip_coef, 1)
                nc.vector.tensor_scalar(gn_b_all[:, :], gn_b_all[:, :], 1.0 / GN_SCALE, None, ALU.mult).then_inc(skip_coef, 1)
                dve.wait_ge(skip_coef, 2)

            def lo_and_last_bn(ph, i, r):
                if r >= 1:
                    bn_stats(ph, i - 1, r - 1, 1)
                if 0 <= r + 1 < NIMG:
                    split_lo(ph, i + 1, r + 1)
                if r >= 1 and r % BODY == 0:
                    bn_accumulate(ph, i - 1, r - 1)

            def pass1(i, r):
                if r % 2 == 0 and r + 3 < NIMG:
                    gn_stats(i + 3, r + 3)
                    gn_pair_a(i + 2, r + 2)
                    bn_stats(0, i - 1, r - 1, 1)
                    gn_pair_b1(i + 2, r + 2)
                else:
                    bn_stats(0, i - 1, r - 1, 1)
                    if r + 3 < NIMG:
                        gn_stats(i + 3, r + 3)
                if r + 1 < NIMG:
                    split_lo(0, i + 1, r + 1)
                if r % 2 == 0 and r + 3 < NIMG:
                    gn_pair_b2(i + 2, r + 2)
                if r % BODY == 0:
                    bn_accumulate(0, i - 1, r - 1)
                if r < NIMG:
                    bn_stats(0, i, r, 0)

            weight_absmax(0)
            for n in range(2):
                setup_step(nc.vector.memset(bn_acc[n][:, :], 0.0))
            quantise(0)
            averages()
            gn_stats(0, 0)
            gn_chain_a(0, 0)
            gn_chain_b1(0, 0)
            gn_chain_b2(0, 0)
            dve.wait_ge(pads_zeroed, PADS_1)
            def start(i, chain_a, chain_b1, chain_b2):
                half_act_x(i)
                gn_stats(i + 1, i + 1, parts=(0,))
                if i >= 2:
                    bn_stats(0, i - 2, i - 2, 1)
                half_lo_x(i)
                gn_stats(i + 1, i + 1, parts=(1, 2, 3))
                if i == ALONE - 1:
                    gn_stats(i + 2, i + 2)
                chain_a(i + 1, i + 1)
                rest_lo(0, i)
                chain_b1(i + 1, i + 1)
                if i >= 1:
                    bn_stats(0, i - 1, i - 1, 0)
                chain_b2(i + 1, i + 1)

            for i in range(ALONE - 1):
                start(i, gn_chain_a, gn_chain_b1, gn_chain_b2)
            start(ALONE - 1, gn_pair_a, gn_pair_b1, gn_pair_b2)
            half_act_x(4)
            bn_stats(0, 2, 2, 1)
            half_lo_x(4)
            gn_stats(6, 6)
            rest_lo(0, 4)
            bn_stats(0, 3, 3, 0)
            run_slots(dve, BODY, NIMG - BODY, pass1)
            run_slots(dve, NIMG - BODY, NIMG - BODY + 1, pass1)
            bn_average()
            weight_absmax(1)
            power_of_two()
            run_slots(dve, NIMG - BODY + 1, NIMG - BODY + 2, pass1)
            quantise(1)
            run_slots(dve, NIMG - BODY + 2, NIMG, pass1)
            conv2_matrix()
            run_slots(dve, NIMG, NIMG + 1, pass1)
            bn_coefficients(0)

            def pass2(i, r):
                lo_and_last_bn(1, i, r)
                if 0 <= r < NIMG:
                    bn_stats(1, i, r, 0)

            dve.wait_ge(bn_coef_ready[0], 1)
            half_lo_y1()
            rest_lo(1, 0)
            run_slots(dve, 0, BODY, pass2)
            run_slots(dve, BODY, NIMG - BODY, pass2)
            skip_coefficients()
            run_slots(dve, NIMG - BODY, NIMG + 1, pass2)
            bn_coefficients(1)

            def pass3(q, r):
                img = image_of(q, r)
                xs = x3_buffer(r)
                if r < OWN:
                    dve.wait_ge(x3_own_loaded[r], 32)
                else:
                    dve.wait_ge(x3_loaded[r % 4], (q - first_use(r % 4)) * 8 + 32)
                u = place(q, r).rearrange("p j w -> p (j w)")

                def columns(cols, u_done, sum_done, done, count):
                    dve.wait_ge(u_done, count)
                    nc.vector.scalar_tensor_tensor(out=u[:, cols], in0=xs[:, cols], scalar=skip_s[:, bass.ds(img, 1)],
                                                   in1=u[:, cols], op0=ALU.mult, op1=ALU.add).then_inc(sum_done, 1)
                    dve.wait_ge(sum_done, count)
                    nc.vector.scalar_tensor_tensor(out=u[:, cols], in0=u[:, cols], scalar=0.0, in1=xs[:, cols],
                                                   op0=ALU.max, op1=ALU.add).then_inc(done, 1)

                if r == 0:
                    columns(slice(0, PIX // 2), half_u, half_sum, half_out, 1)
                    columns(slice(PIX // 2, PIX), u_ready, sum_ready, out_ready, 1)
                else:
                    columns(slice(0, PIX), u_ready, sum_ready, out_ready, q + 1)

            for q in range(RES - BODY):
                pass3(q, q)
            run_slots(dve, RES - BODY, RES, pass3)
            run_slots(dve, RES, NIMG, pass3)

        @block.tensor
        def _(pe):
            pe.wait_ge(masks_made, 1)

            def weight_transposes(n):
                pe.wait_ge(quantised, n + 1)
                for kx in range(3):
                    for pair, o, ky in ((0, 0, 1), (0, 1, 0), (1, 0, 3), (1, 1, 2)):
                        mm = nc.tensor.transpose(wt_ps[n][:, kx, pair, o * C:(o + 1) * C],
                                                 wpad[:, kx, ky:ky + 2, :].rearrange("o a i -> o (a i)"), ident[:, :])
                mm.then_inc(transposed, 1)

            weight_transposes(0)

            def gn_combine(i, r):
                m = r % 2
                pe.wait_ge(gn_moments, i + 1)
                if r >= 2:
                    pe.wait_ge(gn_var_ready, i - 1)
                nc.tensor.matmul(stat_ps[:, 2 * m:2 * m + 2], gn_avg[:, :], gn_mv[:, m, :],
                                 start=True, stop=True).then_inc(gn_combined, 1)

            def gn_combine_pair(i, r):
                pe.wait_ge(gn_moments, i + 2)
                pe.wait_ge(gn_var_ready, i)
                nc.tensor.matmul(stat_ps[:, 0:4], gn_avg[:, :], gn_mv[:, :, :].rearrange("p a b -> p (a b)"),
                                 start=True, stop=True).then_inc(gn_combined, 2)

            TAPS = ((1, 0), (0, 0), (0, 1), (2, 0), (2, 1), (1, 1))
            conv_rows = conv_ps[:, :, 0:CH].rearrange("p c (r w) -> p c r w", w=W)

            def conv(ph, i, r, combine=None, at=None):
                k = r % 2
                halves = r < DIRECT[ph]
                for p in range(NPAIR):
                    if halves and p == 0:
                        pe.wait_ge(half_lo[ph], i + 1)
                    elif halves or p == 0:
                        pe.wait_ge(hi_ready[ph], i + 1)
                        pe.wait_ge(lo_ready[ph], i + 1)
                    if r >= 1:
                        pe.wait_ge(pair_evac[ph][p], i)
                    by_chunk = r == NIMG - 1 and p == 1
                    for chunks in (((2,), (3,)) if by_chunk else ((2 * p, 2 * p + 1),)):
                        for n, (kx, pair) in enumerate(TAPS):
                            w0, w1 = max(0, 1 - kx), min(W, W + 1 - kx)
                            for part in (hi, lo):
                                for c in chunks:
                                    k0 = c * ROWS_PER_BANK + pair
                                    mm = nc.tensor.matmul(conv_rows[:, c, :, w0:w1], wmat[ph][:, kx, pair, :],
                                                          part[:, k, k0:k0 + ROWS_PER_BANK, w0 + kx - 1:w1 + kx - 1],
                                                          start=n == 0 and part is hi, stop=n == 5 and part is lo)
                            if n == 5 and chunks == (2,):
                                mm.then_inc(chunk_done[ph], 1)
                            elif n == 5:
                                mm.then_inc(pair_done[ph][p], 1)
                            if combine and (p, n) == at:
                                combine()

            def pass1(i, r):
                if r % 2 == 0 and r + 2 < NIMG:
                    conv(0, i, r, lambda: gn_combine_pair(i + 2, r + 2), at=(0, 4))
                else:
                    conv(0, i, r)

            def keep_warm(n, count):
                for _ in range(count):
                    nc.tensor.matmul(conv_ps[:, 0, 0:CH], wmat[n][:, 0, 0, :],
                                     wmat[n][:, :, :, :].rearrange("p a b m -> p (a b m)")[:, 0:CH], start=True, stop=True)

            pe.wait_ge(averages_made, 1)
            pe.wait_ge(wmat_ready, 1)
            keep_warm(0, 4)
            gn_combine(0, 0)
            keep_warm(0, 13)
            conv(0, 0, 0, lambda: gn_combine(1, 1), at=(0, 3))
            conv(0, 1, 1, lambda: gn_combine(2, 2), at=(0, 1))
            conv(0, 2, 2, lambda: gn_combine(3, 3), at=(0, 1))
            conv(0, 3, 3, lambda: gn_combine_pair(4, 4), at=(0, 5))
            run_slots(pe, BODY, 2 * BODY, pass1)
            run_slots(pe, 2 * BODY, NIMG - BODY, pass1)
            run_slots(pe, NIMG - BODY, NIMG - 1, pass1)
            weight_transposes(1)
            run_slots(pe, NIMG - 1, NIMG, pass1)

            pe.wait_ge(pair_evac[0][1], NIMG)
            pe.wait_ge(wmat_ready, 2)
            keep_warm(1, 8)

            def bn_combine(ph):
                pe.wait_ge(averages_made, 2)
                pe.wait_ge(bn_sums[ph], NIMG)
                nc.tensor.matmul(stat_ps[:, 0:2], bn_avg[:, :], bn_acc[ph][:, :], start=True, stop=True).then_inc(bn_combined[ph], 1)

            bn_combine(0)
            keep_warm(1, 20)
            run_slots(pe, 0, BODY, lambda i, r: conv(1, i, r))
            run_slots(pe, BODY, NIMG - BODY, lambda i, r: conv(1, i, r))
            run_slots(pe, NIMG - BODY, NIMG, lambda i, r: conv(1, i, r))
            bn_combine(1)


_INS = ['x', 'L0_conv_w1', 'L0_conv_b1', 'L0_conv_gamma1', 'L0_conv_beta1',
        'L0_conv_w2', 'L0_conv_b2', 'L0_conv_gamma2', 'L0_conv_beta2']


def kernel(**inputs):
    import numpy as _np
    import concourse.bacc as _bacc
    from concourse import mybir as _mybir
    from concourse.bass_utils import run_bass_kernel_spmd as _run

    nc = _bacc.Bacc("TRN2", target_bir_lowering=False, num_devices=1)
    arrays, args = {}, []
    for name in _INS:
        a = _np.ascontiguousarray(inputs[name])
        arrays[f"in_{name}_dram"] = a
        args.append(nc.dram_tensor(f"in_{name}_dram", a.shape, _mybir.dt.from_np(a.dtype), kind="ExternalInput").ap())
    shape = inputs["x"].shape
    args.append(nc.dram_tensor("out_0_dram", shape, _mybir.dt.float32, kind="ExternalOutput").ap())
    conv_block_kernel(nc, *args)
    r = _run(nc, [arrays], core_ids=[0])
    return r.results[0]["out_0_dram"]
```
